# Optimizing a Trainium2 kernel written in Bass

```python
import numpy as np
import jax
import jax.numpy as jnp

def _softmax(x, axis=-1):
    return jax.nn.softmax(x, axis=axis)

def _gelu(x):
    return jax.nn.gelu(x, approximate=True)

def _silu(x):
    return jax.nn.silu(x)

def _sigmoid(x):
    return jax.nn.sigmoid(x)

def _layernorm(x, axis=-1, eps=1e-05):
    m = jnp.mean(x, axis=axis, keepdims=True)
    v = jnp.var(x, axis=axis, keepdims=True)
    return (x - m) / jnp.sqrt(v + eps)

def _scatter_add(tgt, idx, src, axis=0):
    return tgt.at[idx].add(src)

def _segment_sum(src, seg, n):
    return jax.ops.segment_sum(src, seg, n)
kernel_name = 'mk_xattn_ffn_d1_seqx_r8_5e642c'

def setup_inputs(seed: int=0):
    np.random.seed(seed)
    _w = jnp.asarray

    def _rec_inputs():
        import jax
        import jax.numpy as jnp
        _rk = jax.random.key(seed)
        x = -0.0005207 + 1.001 * jax.random.normal(jax.random.fold_in(_rk, 1), (1, 1024, 128), jnp.float32)
        _lenS = 1024 - jax.random.randint(jax.random.fold_in(_rk, 7), (1,), 0, max(1, 1024 // 4) + 1, jnp.int32)
        _lenS2 = 6404 - jax.random.randint(jax.random.fold_in(_rk, 8), (1,), 0, max(1, 6404 // 4) + 1, jnp.int32)
        _ctx_1024P = jax.random.normal(jax.random.fold_in(_rk, 11), (1, 16, 128), jnp.float32)
        _ctx_1024c = jax.random.dirichlet(jax.random.fold_in(_rk, 511), 0.3 * jnp.ones((16,), jnp.float32), (1, 6404))
        _ctx_1024t = jnp.einsum('bsk,bkd->bsd', _ctx_1024c, _ctx_1024P)
        _ctx_1024t = _ctx_1024t * jax.lax.rsqrt(jnp.mean(jnp.square(_ctx_1024t)) + 1e-12) * 0.953939
        ctx_1024 = 4.13588e-05 + 0.999923 * (_ctx_1024t + 0.3 * jax.random.normal(jax.random.fold_in(_rk, 611), (1, 6404, 128), jnp.float32))
        _validS = jnp.arange(1024)[None, :] < _lenS[:, None]
        _validS2 = jnp.arange(6404)[None, :] < _lenS2[:, None]
        _causal = jnp.tril(jnp.ones((1024, 1024), dtype=bool))
        mask_BxS2_bk0 = jnp.logical_not(jnp.broadcast_to(_validS2[:, :], (1, 6404)))
        return (x, ctx_1024, mask_BxS2_bk0)
    x, ctx_1024, mask_BxS2_bk0 = _rec_inputs()

    def _L0_xattn_setup():
        import jax, jax.numpy as jnp
        import numpy as np
        DIM = 128
        NUM_HEADS = 16
        HEAD_DIM = DIM // NUM_HEADS
        SCALE = HEAD_DIM ** (-0.5)
        EPS = 1e-05

        def _layernorm(x, w, b):
            mu = jnp.mean(x, axis=-1, keepdims=True)
            var = jnp.mean(jnp.square(x - mu), axis=-1, keepdims=True)
            return (x - mu) * jax.lax.rsqrt(var + EPS) * w + b

        def _split_heads(x):
            B, L, _ = x.shape
            return x.reshape(B, L, NUM_HEADS, HEAD_DIM).transpose(0, 2, 1, 3)
        key = jax.random.key(seed)
        ks = jax.random.split(key, 12)
        B, Lq, Lk = (4, 64, 256)
        inp = {'query': jax.random.normal(ks[0], (B, Lq, DIM), jnp.float32), 'context': jax.random.normal(ks[1], (B, Lk, DIM), jnp.float32), 'context_mask': jax.random.randint(ks[2], (B, Lk), 0, 2).astype(bool), 'qn_w': jnp.ones((DIM,), jnp.float32), 'qn_b': jnp.zeros((DIM,), jnp.float32), 'cn_w': jnp.ones((DIM,), jnp.float32), 'cn_b': jnp.zeros((DIM,), jnp.float32)}
        std = DIM ** (-0.5)
        for i, name in enumerate(['q', 'k', 'v', 'o']):
            inp[f'W{name}'] = jax.random.normal(ks[3 + i], (DIM, DIM), jnp.float32) * std
            inp[f'b{name}'] = jnp.zeros((DIM,), jnp.float32)
        return inp
    _L0_xattn_all = _L0_xattn_setup()
    _L0_xattn_in = {k: v for k, v in _L0_xattn_all.items() if k in ('qn_w', 'qn_b', 'cn_w', 'cn_b', 'Wq', 'bq', 'Wk', 'bk', 'Wv', 'bv', 'Wo', 'bo')}
    del _L0_xattn_all

    def _L0_ffn_setup():
        import jax, jax.numpy as jnp
        import numpy as np
        DIM = 128
        HIDDEN = 256
        N_EXPERTS = 8
        TOP_K = 2
        EPS = 1e-06

        def rms_norm(x, scale, eps=EPS):
            ms = jnp.mean(jnp.square(x.astype(jnp.float32)), axis=-1, keepdims=True)
            s = scale.astype(jnp.float32) * jax.lax.rsqrt(ms + eps)
            return x * s.astype(x.dtype)

        def moe_linear(xf, ids, W):
            E = W.shape[0]
            out = jnp.zeros((xf.shape[0], W.shape[1]), dtype=xf.dtype)
            for e in range(E):
                out = out + jnp.where((ids == e)[:, None], xf @ W[e].T, 0.0)
            return out
        key = jax.random.key(seed)
        k1, k2, k3, k4 = jax.random.split(key, 4)
        x = jax.random.normal(k1, (4, 512, DIM), dtype=jnp.float32)
        norm_scale = jnp.ones((DIM,), dtype=jnp.float32)
        w_router = jax.random.normal(k2, (N_EXPERTS, DIM), dtype=jnp.float32) / np.sqrt(DIM)
        lim_up = np.sqrt(6.0 / (DIM + 2 * HIDDEN))
        w_up = jax.random.uniform(k3, (N_EXPERTS, 2 * HIDDEN, DIM), dtype=jnp.float32, minval=-lim_up, maxval=lim_up)
        lim_dn = np.sqrt(6.0 / (HIDDEN + DIM))
        w_down = jax.random.uniform(k4, (N_EXPERTS, DIM, HIDDEN), dtype=jnp.float32, minval=-lim_dn, maxval=lim_dn)
        return {'x': x, 'norm_scale': norm_scale, 'w_router': w_router, 'w_up': w_up, 'w_down': w_down}
    _L0_ffn_all = _L0_ffn_setup()
    _L0_ffn_in = {k: v for k, v in _L0_ffn_all.items() if k in ('norm_scale', 'w_router', 'w_up', 'w_down')}
    del _L0_ffn_all
    return {'x': x, 'ctx_1024': ctx_1024, 'mask_BxS2_bk0': mask_BxS2_bk0, 'L0_xattn_qn_w': _L0_xattn_in['qn_w'], 'L0_xattn_qn_b': _L0_xattn_in['qn_b'], 'L0_xattn_cn_w': _L0_xattn_in['cn_w'], 'L0_xattn_cn_b': _L0_xattn_in['cn_b'], 'L0_xattn_Wq': _L0_xattn_in['Wq'], 'L0_xattn_bq': _L0_xattn_in['bq'], 'L0_xattn_Wk': _L0_xattn_in['Wk'], 'L0_xattn_bk': _L0_xattn_in['bk'], 'L0_xattn_Wv': _L0_xattn_in['Wv'], 'L0_xattn_bv': _L0_xattn_in['bv'], 'L0_xattn_Wo': _L0_xattn_in['Wo'], 'L0_xattn_bo': _L0_xattn_in['bo'], 'L0_ffn_norm_scale': _L0_ffn_in['norm_scale'], 'L0_ffn_w_router': _L0_ffn_in['w_router'], 'L0_ffn_w_up': _L0_ffn_in['w_up'], 'L0_ffn_w_down': _L0_ffn_in['w_down']}

def reference(x, ctx_1024, mask_BxS2_bk0, L0_xattn_qn_w, L0_xattn_qn_b, L0_xattn_cn_w, L0_xattn_cn_b, L0_xattn_Wq, L0_xattn_bq, L0_xattn_Wk, L0_xattn_bk, L0_xattn_Wv, L0_xattn_bv, L0_xattn_Wo, L0_xattn_bo, L0_ffn_norm_scale, L0_ffn_w_router, L0_ffn_w_up, L0_ffn_w_down):
    import jax
    import jax.numpy as jnp

    def _L0_xattn_ref(query, context, context_mask, qn_w, qn_b, cn_w, cn_b, Wq, bq, Wk, bk, Wv, bv, Wo, bo):
        import jax, jax.numpy as jnp
        import numpy as np
        DIM = 128
        NUM_HEADS = 16
        HEAD_DIM = DIM // NUM_HEADS
        SCALE = HEAD_DIM ** (-0.5)
        EPS = 1e-05

        def _layernorm(x, w, b):
            mu = jnp.mean(x, axis=-1, keepdims=True)
            var = jnp.mean(jnp.square(x - mu), axis=-1, keepdims=True)
            return (x - mu) * jax.lax.rsqrt(var + EPS) * w + b

        def _split_heads(x):
            B, L, _ = x.shape
            return x.reshape(B, L, NUM_HEADS, HEAD_DIM).transpose(0, 2, 1, 3)
        B, Lq, _ = query.shape
        fully_masked = jnp.all(context_mask, axis=1)
        mask = context_mask.at[:, 0].set(jnp.where(fully_masked, False, context_mask[:, 0]))
        qn = _layernorm(query, qn_w, qn_b)
        cn = _layernorm(context, cn_w, cn_b)
        q = _split_heads(qn @ Wq.T + bq)
        k = _split_heads(cn @ Wk.T + bk)
        v = _split_heads(cn @ Wv.T + bv)
        logits = jnp.einsum('bhqd,bhkd->bhqk', q * SCALE, k)
        logits = jnp.where(mask[:, None, None, :], -jnp.inf, logits)
        attn = jax.nn.softmax(logits, axis=-1)
        out = jnp.einsum('bhqk,bhkd->bhqd', attn, v)
        out = out.transpose(0, 2, 1, 3).reshape(B, Lq, DIM)
        return out @ Wo.T + bo

    def _L0_ffn_ref(x, norm_scale, w_router, w_up, w_down):
        import jax, jax.numpy as jnp
        import numpy as np
        DIM = 128
        HIDDEN = 256
        N_EXPERTS = 8
        TOP_K = 2
        EPS = 1e-06

        def rms_norm(x, scale, eps=EPS):
            ms = jnp.mean(jnp.square(x.astype(jnp.float32)), axis=-1, keepdims=True)
            s = scale.astype(jnp.float32) * jax.lax.rsqrt(ms + eps)
            return x * s.astype(x.dtype)

        def moe_linear(xf, ids, W):
            E = W.shape[0]
            out = jnp.zeros((xf.shape[0], W.shape[1]), dtype=xf.dtype)
            for e in range(E):
                out = out + jnp.where((ids == e)[:, None], xf @ W[e].T, 0.0)
            return out
        B, S, D = x.shape
        skip = x
        xn = rms_norm(x, norm_scale)
        scores = (xn @ w_router.T).astype(jnp.float32)
        scores_topk, idx = jax.lax.top_k(scores, TOP_K)
        weights = jax.nn.softmax(scores_topk, axis=-1)
        xf = jnp.broadcast_to(xn[..., None, :], (B, S, TOP_K, D)).reshape(-1, D)
        ids = idx.reshape(-1)
        up = moe_linear(xf, ids, w_up)
        u, gate = jnp.split(up, 2, axis=-1)
        h = u * jax.nn.silu(gate)
        down = moe_linear(h, ids, w_down)
        down = down.reshape(B, S, TOP_K, D)
        out = jnp.sum(down * weights[..., None].astype(down.dtype), axis=-2)
        return out + skip
    x = x + _L0_xattn_ref(_layernorm(x, axis=-1), ctx_1024, mask_BxS2_bk0, L0_xattn_qn_w, L0_xattn_qn_b, L0_xattn_cn_w, L0_xattn_cn_b, L0_xattn_Wq, L0_xattn_bq, L0_xattn_Wk, L0_xattn_bk, L0_xattn_Wv, L0_xattn_bv, L0_xattn_Wo, L0_xattn_bo)
    x = x + _L0_ffn_ref(_layernorm(x, axis=-1), L0_ffn_norm_scale, L0_ffn_w_router, L0_ffn_w_up, L0_ffn_w_down)
    return x

_drawn_inputs = setup_inputs


def setup_inputs(seed=0):
    import zlib

    import numpy as np

    out = dict(_drawn_inputs(seed))
    spreads = {'L0_xattn_qn_w': (1.0, 0.2),
     'L0_xattn_qn_b': (0.0, 0.414),
     'L0_xattn_cn_w': (1.0, 0.2),
     'L0_xattn_cn_b': (0.0, 0.1),
     'L0_xattn_bq': (0.0, 0.454),
     'L0_xattn_bk': (0.0, 0.8),
     'L0_xattn_bv': (0.0, 0.1),
     'L0_xattn_bo': (0.0, 0.1),
     'L0_ffn_norm_scale': (1.0, 0.2)}
    factors = {}
    for name, (base, spread) in spreads.items():
        noise = np.random.default_rng([zlib.crc32(name.encode()), seed]).standard_normal(out[name].shape)
        drawn = base * np.exp(spread * noise) if base else spread * noise
        out[name] = jnp.asarray(drawn.astype(out[name].dtype))
    for name, factor in factors.items():
        out[name] = (out[name] * factor).astype(out[name].dtype)
    return out
```

```python
from contextlib import ExitStack

import numpy as np

import concourse.bass as bass
from concourse import mybir
from concourse.alu_op_type import AluOpType as ALU

F32 = mybir.dt.float32
BF16 = mybir.dt.bfloat16
I32 = mybir.dt.int32
U8 = mybir.dt.uint8
U32 = mybir.dt.uint32
ACT = mybir.ActivationFunctionType
AX_X = mybir.AxisListType.X

P = 128
QUERIES, KEYS, DIM, HEADS = 1024, 6404, 128, 16
HEAD = DIM // HEADS
SCALE = HEAD ** -0.5
EXPERTS, HIDDEN = 8, 256
EPS_LN, EPS_RMS = 1e-5, 1e-6
BANK = 512
QT = QUERIES // P
QC = QUERIES // BANK
CHUNKS = -(-KEYS // BANK)
KT = CHUNKS * 4
ATT_T = -(-KEYS // P)
ATT_K = ATT_T * P
STEP_T = 3
STEPS = ATT_T // STEP_T
PAIRS = HEADS // 2
UNITS = 4
GROUP = 3
GROUPS = STEP_T * UNITS // GROUP
GW = GROUP * BANK
PARTS = 3
VW = HEAD + 1
ROW_MASK, ROW_SHIFT = 96, 97
MASKED = -1e30
GAP_LIMIT = 60.0
STAT_GROUPS = 4
STAT_T = KT // STAT_GROUPS
assert ATT_T % STEP_T == 0 and KT % STAT_GROUPS == 0 and PARTS * PARTS * HEAD <= ROW_MASK

C_IDENT, C_BLOCK, C_IOTA = 0, P, P + HEADS
C_W = C_IOTA + EXPERTS
W_Q, W_K, W_V, W_O, W_R = 0, DIM, 2 * DIM, 3 * DIM, 4 * DIM
W_W = W_R + EXPERTS
COLS = ["qn_w", "qn_b", "cn_w", "cn_b", "bq", "bk", "bv", "ns"]


def build(nc, x, ctx, mask, consts, weights, cols, bo, w_up, w_down, out, gap_limit=GAP_LIMIT):
    kparts_dram = nc.dram_tensor("kparts_dram", [HEADS, PARTS * HEAD, KT * P], BF16).ap()
    qparts_dram = nc.dram_tensor("qparts_dram", [PARTS, DIM, QUERIES], BF16).ap()
    attn_dram = nc.dram_tensor("attn_dram", [HEADS + 2, VW, QUERIES], F32).ap()

    with ExitStack() as es:
        def sb(name, shape, dt=F32):
            return es.enter_context(nc.sbuf_tensor(name, shape, dt))

        def sem(name):
            return es.enter_context(nc.semaphore(name))

        banks = es.enter_context(nc.psum_tensor("banks", [P, 8, BANK], F32))

        con = sb("con", [P, C_W])
        wts = sb("wts", [P, W_W])
        col = sb("col", [P, len(COLS)])
        bo_b = sb("bo_b", [P, DIM])
        x_in = sb("x_in", [P, QT, DIM])
        ctx_in = sb("ctx_in", [P, KT, DIM])
        wdown = sb("wdown", [P, EXPERTS + 1, 2, DIM])
        v_all = sb("v_all", [P, KT, HEADS, VW])
        kaug = sb("kaug", [P, 2, 2, ATT_K], BF16)
        qaug = sb("qaug", [P, HEADS, QUERIES], BF16)
        probs = sb("probs", [P, STEP_T * UNITS * BANK])
        v_step = sb("v_step", [P, STEP_T, 2, VW])
        z = sb("z", [P, 2, 4, P])
        nT = sb("nT", [P, 2, BANK])
        wup = nT
        kf = sb("kf", [P, 2, BANK])
        rest = sb("rest", [P, BANK])
        mask_f = rest[0:KT, 0:P]
        kpart = sb("kpart", [P, 2, PARTS, BANK], BF16)
        kmax = sb("kmax", [P, BANK], BF16)
        kmin = sb("kmin", [P, BANK], BF16)
        st6 = sb("st6", [P, KT, 6])
        mean = sb("mean", [P, KT])
        tmp = sb("tmp", [P, 4, KT])
        sd = sb("sd", [P, KT])
        rstd = sb("rstd", [P, KT])
        neg = sb("neg", [P, KT])
        small = sb("small", [P, 16])
        bnd = sb("bnd", [P, 4, HEADS])
        mask_u8 = sb("mask_u8", [KT, P], U8)
        mask_row = sb("mask_row", [KT, P], BF16)
        flag = sb("flag", [1, 2], I32)

        free = ctx_in[:].rearrange("p t d -> p (t d)")
        shift, shift_rest = free[0:HEADS, 0:QUERIES], free[0:HEADS, QUERIES:2 * QUERIES]
        shift_part = free[0:HEADS, 2 * QUERIES:4 * QUERIES].bitcast(BF16)[:, 0:PARTS * QUERIES].rearrange(
            "h (a n) -> h a n", a=PARTS)
        o_sb = free[:, 4 * QUERIES:5 * QUERIES].rearrange("p (s n) -> p s n", s=2)
        r_sb = free[:, 5 * QUERIES:6 * QUERIES].rearrange("p (s n) -> p s n", s=2)
        qmax = free[:, 6 * QUERIES:6 * QUERIES + QT * HEADS].rearrange("p (t h) -> p t h", h=HEADS)
        def probs_view(k, n=QUERIES):
            return probs[:, k * QUERIES:k * QUERIES + n]
        q_pos, q_neg, qT, q_rest = (probs_view(k) for k in range(4))
        LATE = 2 * QUERIES
        qpart = probs[:, 4 * QUERIES:6 * QUERIES].bitcast(BF16)[:, 0:PARTS * QUERIES].rearrange(
            "p (a n) -> p a n", a=PARTS)
        late = kaug[:].rearrange("p a b n -> p (a b n)").bitcast(F32)

        def late_view(k):
            return late[:, k * QUERIES:(k + 1) * QUERIES]
        den_b, attn_raw, attnT, x1, zf, acc, xs, xnT, hT_all, sg_all = (late_view(k) for k in range(10))
        tiles = lambda v: v.rearrange("p (t d) -> p t d", d=DIM)
        hT = [late_view(8).rearrange("p (j n) -> p j n", j=2), late_view(10).rearrange("p (j n) -> p j n", j=2)]
        sg = sg_all.rearrange("p (b n) -> p b n", b=2)
        sc8 = sb("sc8", [P, QT, 8])
        top8 = sb("top8", [P, QT, 8])
        idx8 = sb("idx8", [P, QT, 8], U32)
        idxf = sb("idxf", [P, QT, 2])
        wt2 = sb("wt2", [P, QT, 4])
        pick = sb("pick", [P, 2, QT, EXPERTS])
        gate = sb("gate", [P, QT, EXPERTS + 1])

        def W(at, n=DIM):
            return wts[:, at:at + n]

        def C(name):
            i = COLS.index(name)
            return col[:, i:i + 1]
        ident = con[:, C_IDENT:C_IDENT + P]
        block = con[:, C_BLOCK:C_BLOCK + HEADS]
        iota8 = con[:, C_IOTA:C_IOTA + EXPERTS]
        eps_ln, eps_rms = small[:, 0:1], small[:, 1:2]

        small_loaded = sem("small_loaded")
        x_loaded = sem("x_loaded")
        mask_loaded = sem("mask_loaded")
        ctx_loaded = [sem(f"ctx_loaded{g}") for g in range(STAT_GROUPS)]
        experts_loaded = sem("experts_loaded")
        consts_set = sem("consts_set")
        vchain = sem("vchain")
        pchain = sem("pchain")
        var_ready = sem("var_ready")
        sd_ready = sem("sd_ready")
        zq_ready = sem("zq_ready")
        zq_turned = sem("zq_turned")
        qn_ready = sem("qn_ready")
        q_projected = sem("q_projected")
        q_ready = sem("q_ready")
        qpart_ready = sem("qpart_ready")
        qparts_stored = sem("qparts_stored")
        qaug_zeroed = sem("qaug_zeroed")
        qaug_loaded = sem("qaug_loaded")
        z_scaled = sem("z_scaled")
        z_ready = sem("z_ready")
        turned = sem("turned")
        n_ready = sem("n_ready")
        projected = sem("projected")
        part1_ready = sem("part1_ready")
        evacuated = sem("evacuated")
        parts_made = sem("parts_made")
        neg_ready = sem("neg_ready")
        probs_cleared = sem("probs_cleared")
        kparts_stored = [sem(f"kparts_stored{b}") for b in range(2)]
        chunks_stored = sem("chunks_stored")
        kaug_set = sem("kaug_set")
        mask_counted = sem("mask_counted")
        mask_summed = sem("mask_summed")
        mask_ready = sem("mask_ready")
        fixed_rows = sem("fixed_rows")
        bnd_ready = sem("bnd_ready")
        bound_summed = sem("bound_summed")
        gap_summed = sem("gap_summed")
        gap_ready = sem("gap_ready")
        gap_turned = sem("gap_turned")
        flag_ready = sem("flag_ready")
        max_keys_loaded = sem("max_keys_loaded")
        max_scores_ready = sem("max_scores_ready")
        max_taken = sem("max_taken")
        max_pair_done = sem("max_pair_done")
        max_found = sem("max_found")
        max_turned = sem("max_turned")
        max_split = sem("max_split")
        max_ready = sem("max_ready")
        shift_ready = sem("shift_ready")
        shift_loaded = sem("shift_loaded")
        keys_loaded = [sem(f"keys_loaded{s}") for s in range(2)]
        pair_started = sem("pair_started")
        scores_ready = sem("scores_ready")
        probs_ready = sem("probs_ready")
        v_staged = sem("v_staged")
        step_summed = sem("step_summed")
        o_copied = sem("o_copied")
        o_floored = sem("o_floored")
        bias_projected = sem("bias_projected")
        o_stored = [sem(f"o_stored{s}") for s in range(2)]
        sums_ready = sem("sums_ready")
        attn_loaded = [sem(f"attn_loaded{c}") for c in range(QC)]
        attn_ready = sem("attn_ready")
        out_projected = sem("out_projected")
        zf_ready = sem("zf_ready")
        squares_ready = sem("squares_ready")
        xs_ready = sem("xs_ready")
        xs_turned = sem("xs_turned")
        xn_ready = sem("xn_ready")
        routed = sem("routed")
        top_ready = sem("top_ready")
        ratio_ready = sem("ratio_ready")
        wup_loaded = [sem(f"wup_loaded{s}") for s in range(2)]
        up_gate_ready = sem("up_gate_ready")
        up_ready = sem("up_ready")
        silu_ready = sem("silu_ready")
        h_ready = sem("h_ready")
        down_ready = sem("down_ready")
        acc_done = sem("acc_done")
        out_stored = sem("out_stored")

        dram_tiles = lambda a: a.rearrange("(t p) d -> p t d", p=P)
        KAUG_DMAS = 2
        STORE = 2 * UNITS * 16
        KSTORE = PARTS * 16

        def load_keys(eng, pair, slot, done, first=0, n=ATT_K):
            for hh in range(2):
                src = kparts_dram[bass.ds(2 * pair + hh, 1), :, bass.ds(first, n)]
                eng.dma_start(kaug[0:PARTS * PARTS * HEAD, slot, hh, bass.ds(first, n)],
                              src.to_broadcast([PARTS, PARTS * HEAD, n])).then_inc(done, 16)

        BODY_CHUNKS = CHUNKS - 1
        LEAD = 2

        def passed(i):
            return i + 1

        def through(i):
            return i + 1 + LEAD

        blk = es.enter_context(nc.Block())

        @blk.sync
        def _(sp):
            for b in range(2):
                sp.sem_inc(kparts_stored[b], KSTORE)
            sp.dma_start(x_in[:], dram_tiles(x)).then_inc(x_loaded, 16)
            for dst, src in ((con[:], consts), (wts[:], weights), (col[:], cols),
                             (bo_b[:], bo.partition_broadcast(P))):
                sp.dma_start(dst, src).then_inc(small_loaded, 16)
            sp.dma_start(mask_u8[:], mask).then_inc(mask_loaded, 16)
            ct = dram_tiles(ctx)
            for g in range(STAT_GROUPS):
                sp.dma_start(ctx_in[:, g * STAT_T:(g + 1) * STAT_T, :],
                             ct[:, g * STAT_T:(g + 1) * STAT_T, :]).then_inc(ctx_loaded[g], 16)
            sp.wait_ge(qpart_ready, 3)
            sp.dma_start(qparts_dram.rearrange("a f n -> f a n"), qpart).then_inc(qparts_stored, 16)
            sp.wait_ge(qparts_stored, 16)
            sp.wait_ge(qaug_zeroed, 2)
            for a in range(PARTS):
                for b in range(PARTS):
                    r = (a * PARTS + b) * HEAD
                    sp.dma_start(qaug[r:r + HEAD, :, :],
                                 qparts_dram[a].rearrange("(h d) n -> d h n", d=HEAD)).then_inc(qaug_loaded, 16)
            sp.wait_ge(kaug_set, 1)
            sp.wait_ge(mask_ready, 1)
            for s in range(2):
                for hh in range(2):
                    sp.dma_start(kaug[ROW_MASK:ROW_MASK + 1, s, hh, :],
                                 mask_row[0:ATT_T, :]).then_inc(fixed_rows, 16)

            def store_kparts(i, b):
                for part in range(PARTS):
                    sp.wait_ge(parts_made, PARTS * through(i) - PARTS + part + 1)
                    rows = slice(part * HEAD, (part + 1) * HEAD)
                    sp.dma_start(kparts_dram[:, rows, bass.ds(i * BANK, BANK)], kpart[:, b, part, :])\
                      .then_inc(kparts_stored[b], 16)

            def load_chunk(i, j, b, n=BANK):
                sp.wait_ge(kparts_stored[b], KSTORE * (j + 2))
                sp.sem_inc(chunks_stored, 1)
                load_keys(sp, 0, 0, keys_loaded[0], i * BANK, n)
            store_kparts(0, 0)
            with sp.Fori(0, BODY_CHUNKS // 2) as j:
                for b in range(2):
                    store_kparts(2 * j + b + 1, 1 - b)
                    load_chunk(2 * j + b, j, b)
            load_chunk(BODY_CHUNKS, BODY_CHUNKS // 2, 0, ATT_K - BODY_CHUNKS * BANK)
            sp.wait_ge(chunks_stored, CHUNKS)
            for s in range(2):
                sp.dma_start(wup[:, s, :], w_up[s]).then_inc(wup_loaded[s], 16)
            sp.dma_start(wdown[:, 1:, :, :], w_down).then_inc(experts_loaded, 16)
            sp.wait_ge(flag_ready, 1)
            bounded = sp.value_load(flag[0:1, 0:1], min_val=0, max_val=1)
            with sp.If(bounded == 0):
                with sp.Fori(0, PAIRS) as pair:
                    sp.wait_ge(max_pair_done, pair + 1)
                    load_keys(sp, pair, 1, max_keys_loaded)
                sp.wait_ge(max_pair_done, PAIRS + 1)
            load_keys(sp, 1, 1, keys_loaded[1])
            sp.wait_ge(shift_ready, 1)
            for a in range(PARTS):
                sp.dma_start(qaug[ROW_SHIFT + a:ROW_SHIFT + a + 1, :, :], shift_part[:, a, :])\
                  .then_inc(shift_loaded, 16)

            def store_sums(pair, s):
                sp.wait_ge(sums_ready, pair + 1)
                for g in range(UNITS):
                    head, n, at = bass.ds(2 * pair + g // QC, 1), slice(g % QC * BANK, (g % QC + 1) * BANK), 32 * g
                    sp.dma_start(attn_dram[head, 0:HEAD, n], o_sb[at:at + HEAD, s, :]).then_inc(o_stored[s], 16)
                    sp.dma_start(attn_dram[head, HEAD:VW, n], r_sb[at + HEAD:at + VW, s, :]).then_inc(o_stored[s], 16)

            def reload_keys(pair, s):
                sp.wait_ge(pair_started, pair)
                load_keys(sp, pair, s, keys_loaded[s])
            store_sums(0, 0)
            with sp.Fori(0, PAIRS // 2 - 1) as j:
                store_sums(2 * j + 1, 1)
                reload_keys(2 * j + 2, 0)
                store_sums(2 * j + 2, 0)
                reload_keys(2 * j + 3, 1)
            store_sums(PAIRS - 1, 1)
            store_sums(PAIRS, 0)
            for s in range(2):
                sp.wait_ge(o_stored[s], STORE * (PAIRS // 2 + 2 - s))
            for c in range(QC):
                n = slice(c * BANK, (c + 1) * BANK)
                sp.dma_start(attn_raw[:, n], attn_dram[2:, 0:HEAD, n]).then_inc(attn_loaded[c], 16)
                sp.dma_start(den_b[:, n], attn_dram[2:, HEAD:VW, n].to_broadcast([HEADS, HEAD, BANK]))\
                  .then_inc(attn_loaded[c], 16)
            with sp.Fori(1, EXPERTS // 2) as j:
                for s in range(2):
                    sp.wait_ge(up_ready, 2 * QC * (2 * j + s - 1))
                    sp.dma_start(wup[:, s, :], w_up[2 * j + s]).then_inc(wup_loaded[s], 16)
            for half in range(2):
                sp.wait_ge(acc_done, half + 1)
                n = slice(half * 4, half * 4 + 4)
                sp.dma_start(dram_tiles(out)[:, n, :], tiles(acc)[:, n, :]).then_inc(out_stored, 16)
            sp.wait_ge(out_stored, 32)

        @blk.gpsimd
        def _(pool):
            links = [0]

            def chain(ins):
                links[0] += 1
                ins.then_inc(pchain, 1)
                pool.wait_ge(pchain, links[0])

            two_ones = float(np.array([0x3F803F80], np.uint32).view(np.float32)[0])
            chain(pool.memset(qaug[64:P, :, :].bitcast(F32), 0.0))
            pool.memset(qaug[ROW_MASK:ROW_MASK + 1, :, :].bitcast(F32), two_ones).then_inc(qaug_zeroed, 2)
            pool.wait_ge(qaug_zeroed, 2)
            pool.memset(kaug[64:P, :, :, :].bitcast(F32), two_ones).then_inc(kaug_set, 1)
            pool.wait_ge(kaug_set, 1)
            pool.wait_ge(neg_ready, 1)

            def norm_chunk(i, b):
                pool.wait_ge(turned, passed(i))
                each = [P, 4, DIM]
                pool.tensor_tensor(z[:, b, :, :], ctx_in[:, bass.ds(4 * i, 4), :],
                                   rstd[:, bass.ds(4 * i, 4)].unsqueeze(2).to_broadcast(each), ALU.mult)\
                    .then_inc(z_scaled, 1)
                pool.wait_ge(z_scaled, i + 1)
                ins = pool.tensor_tensor(z[:, b, :, :], z[:, b, :, :],
                                         neg[:, bass.ds(4 * i, 4)].unsqueeze(2).to_broadcast(each), ALU.add)
                ins.then_inc(z_ready, 1)
            with pool.Fori(0, BODY_CHUNKS // 2) as j:
                for b in range(2):
                    norm_chunk(2 * j + b, b)
            norm_chunk(BODY_CHUNKS, 0)
            pool.wait_ge(qparts_stored, 16)
            pool.memset(probs[:, LATE:], 0.0).then_inc(probs_cleared, 1)

        @blk.scalar
        def _(act):
            act.sem_inc(n_ready, LEAD)
            act.sem_inc(evacuated, LEAD)
            act.wait_ge(consts_set, 2)
            for n in range(2):
                act.wait_ge(var_ready, n + 1)
                nc.scalar.activation(sd[:, 0:QT], tmp[:, 0, 0:QT], ACT.Sqrt, bias=eps_ln, scale=1.0 / DIM)\
                  .then_inc(sd_ready, 1)
            act.wait_ge(small_loaded, 64)
            for c in range(QC):
                act.wait_ge(zq_turned, c + 1)
                nc.scalar.activation(nT[:, c, :], banks[:, c, :], ACT.Identity, bias=C("qn_b"), scale=C("qn_w"))\
                  .then_inc(qn_ready, 1)
            for c in range(QC):
                act.wait_ge(q_projected, c + 1)
                nc.scalar.activation(qT[:, c * BANK:(c + 1) * BANK], banks[:, 2 + c, :], ACT.Identity, bias=C("bq"))\
                  .then_inc(q_ready, 1)

            for g in range(STAT_GROUPS):
                act.wait_ge(var_ready, 3 + g)
                s = slice(g * STAT_T, (g + 1) * STAT_T)
                nc.scalar.activation(sd[:, s], tmp[:, 0, s], ACT.Sqrt, bias=eps_ln, scale=1.0 / DIM)\
                  .then_inc(sd_ready, 1)

            def affine(i, b):
                act.wait_ge(turned, through(i))
                act.wait_ge(projected, passed(i))
                nc.scalar.activation(nT[:, b, :], banks[:, b, :], ACT.Identity, bias=C("cn_b"), scale=C("cn_w"))\
                  .then_inc(n_ready, 1)

            def evacuate(i, j, b):
                act.wait_ge(projected, through(i))
                act.wait_ge(parts_made, PARTS * passed(i))
                nc.scalar.activation(kf[:, b, :], banks[:, 2 + b, :], ACT.Identity, bias=C("bk"))
                act.wait_ge(kparts_stored[b], KSTORE * (j + 1))
                nc.scalar.activation(kpart[:, b, 0, :], banks[:, 2 + b, :], ACT.Identity, bias=C("bk"))\
                  .then_inc(part1_ready, 1)
                nc.scalar.activation(v_all[:, bass.ds(4 * i, 4), :, 0:HEAD],
                                     banks[:, 4 + b, :].rearrange("p (t h d) -> p t h d", t=4, d=HEAD),
                                     ACT.Copy).then_inc(evacuated, 1)
            affine(0, 0)
            with act.Fori(0, BODY_CHUNKS // 2) as j:
                for b in range(2):
                    affine(2 * j + b + 1, 1 - b)
                    evacuate(2 * j + b, j, b)
            evacuate(BODY_CHUNKS, BODY_CHUNKS // 2, 0)

            act.preload_act_table(ACT.Exp)
            with act.Fori(0, PAIRS * STEPS) as it:
                for g in range(GROUPS):
                    s = GROUP * (g % 2)
                    act.wait_ge(scores_ready, GROUPS * it + g + 1)
                    nc.scalar.activation(probs[:, g * GW:(g + 1) * GW].rearrange("p (b n) -> p b n", n=BANK),
                                         banks[:, s:s + GROUP, :], ACT.Exp, scale=SCALE).then_inc(probs_ready, 1)

            act.wait_ge(var_ready, 3 + STAT_GROUPS)
            nc.scalar.activation(sd[:, 0:QT], tmp[:, 0, 0:QT], ACT.Sqrt, bias=eps_ln, scale=1.0 / DIM)\
              .then_inc(sd_ready, 1)
            act.wait_ge(squares_ready, 1)
            nc.scalar.activation(sd[:, QT:2 * QT], tmp[:, 2, 0:QT], ACT.Sqrt, bias=eps_rms, scale=1.0 / DIM)\
              .then_inc(sd_ready, 1)
            for c in range(QC):
                act.wait_ge(xs_turned, c + 1)
                nc.scalar.activation(xnT[:, c * BANK:(c + 1) * BANK], banks[:, 2 + c, :], ACT.Copy, scale=C("ns"))\
                  .then_inc(xn_ready, 1)
            act.wait_ge(top_ready, 1)
            nc.scalar.activation(wt2[:, :, 1], wt2[:, :, 0], ACT.Exp).then_inc(ratio_ready, 1)
            act.preload_act_table(ACT.Silu)
            with act.Fori(0, 2 * EXPERTS) as r:
                for u in range(2):
                    act.wait_ge(up_gate_ready, 2 * r + u + 1)
                    nc.scalar.activation(sg[:, u, :], banks[:, 2 * u + 1, :], ACT.Silu).then_inc(silu_ready, 1)

        @blk.vector
        def _(dve):
            links = [0]

            def chain(ins):
                links[0] += 1
                ins.then_inc(vchain, 1)
                dve.wait_ge(vchain, links[0])

            dve.memset(eps_ln, EPS_LN).then_inc(consts_set, 1)
            dve.memset(eps_rms, EPS_RMS).then_inc(consts_set, 1)
            dve.sem_inc(parts_made, PARTS * LEAD)
            dve.sem_inc(o_stored[0], STORE)
            dve.sem_inc(o_stored[1], STORE)

            def moments(at, cnt):
                s = slice(at, at + cnt)
                me, ve, mo, vo = (st6[:, s, k] for k in (1, 2, 4, 5))
                nc.vector.tensor_tensor(tmp[:, 0, s], ve, vo, ALU.add)
                nc.vector.tensor_tensor(tmp[:, 1, s], me, mo, ALU.add)
                chain(nc.vector.tensor_tensor(tmp[:, 2, s], me, mo, ALU.subtract))
                nc.vector.tensor_scalar(mean[:, s], tmp[:, 1, s], 0.5, None, ALU.mult)
                chain(nc.vector.scalar_tensor_tensor(tmp[:, 3, s], tmp[:, 2, s], DIM / 4.0, tmp[:, 2, s],
                                                     ALU.mult, ALU.mult))
                nc.vector.tensor_tensor(tmp[:, 0, s], tmp[:, 0, s], tmp[:, 3, s], ALU.add).then_inc(var_ready, 1)

            def x_stats(src):
                for t in range(QT):
                    ins = nc.vector.bn_stats(st6[:, t, :], src[:, t, :])
                chain(ins)
                moments(0, QT)

            def normed(src, dst, done=None, each=None):
                for t in range(QT):
                    ins = nc.vector.tensor_scalar(dst[:, t, :], src[:, t, :], mean[:, t:t + 1], rstd[:, t:t + 1],
                                                  ALU.subtract, ALU.mult)
                    if each is not None and t % 4 == 3:
                        ins.then_inc(each, 1)
                return ins

            dve.wait_ge(x_loaded, 16)
            zq = tiles(q_rest)
            x_stats(x_in)
            dve.wait_ge(sd_ready, 1)
            chain(nc.vector.reciprocal(rstd[:, 0:QT], sd[:, 0:QT]))
            chain(normed(x_in, zq))
            x_stats(zq)
            dve.wait_ge(sd_ready, 2)
            chain(nc.vector.reciprocal(rstd[:, 0:QT], sd[:, 0:QT]))
            normed(zq, tiles(q_pos), each=zq_ready)
            dve.wait_ge(mask_loaded, 16)
            chain(nc.vector.tensor_copy(mask_f, mask_u8[:]))
            chain(nc.vector.tensor_reduce(small[0:KT, 2:3], mask_f, AX_X, ALU.add))
            nc.vector.memset(kmax[:], -3e38)
            nc.vector.memset(kmin[:], 3e38)
            nc.vector.memset(small[:, 3:4], 1.0).then_inc(mask_counted, 1)
            dve.wait_ge(mask_summed, 1)
            chain(nc.vector.tensor_scalar(small[0:1, 4:5], banks[0:1, 7, 0:1], KT * P - 0.5, None, ALU.is_lt))
            chain(nc.vector.tensor_tensor(mask_f[0:1, 0:1], mask_f[0:1, 0:1], small[0:1, 4:5], ALU.mult))
            nc.vector.tensor_scalar(mask_row[:], mask_f, MASKED, None, ALU.mult).then_inc(mask_ready, 1)
            for g in range(STAT_GROUPS):
                dve.wait_ge(ctx_loaded[g], 16)
                for t in range(g * STAT_T, (g + 1) * STAT_T):
                    ins = nc.vector.bn_stats(st6[:, t, :], ctx_in[:, t, :])
                chain(ins)
                moments(g * STAT_T, STAT_T)
            for g in range(STAT_GROUPS):
                dve.wait_ge(sd_ready, 3 + g)
            chain(nc.vector.reciprocal(rstd[:], sd[:]))
            nc.vector.scalar_tensor_tensor(neg[:], mean[:], -1.0, rstd[:], ALU.mult, ALU.mult).then_inc(neg_ready, 1)
            nc.vector.memset(v_all[:, :, :, HEAD:VW], 1.0)

            def split_chunk(i, j, b):
                dve.wait_ge(part1_ready, i + 1)
                dve.wait_ge(parts_made, PARTS * through(i - 1))
                nc.vector.tensor_tensor(rest[:], kf[:, b, :], kpart[:, b, 0, :], ALU.subtract).then_inc(parts_made, 1)
                nc.vector.tensor_tensor(kmax[:], kmax[:], kpart[:, b, 0, :], ALU.max)
                nc.vector.tensor_tensor(kmin[:], kmin[:], kpart[:, b, 0, :], ALU.min)
                dve.wait_ge(parts_made, PARTS * through(i) - 2)
                nc.vector.tensor_copy(kpart[:, b, 1, :], rest[:]).then_inc(parts_made, 1)
                dve.wait_ge(parts_made, PARTS * through(i) - 1)
                nc.vector.tensor_tensor(kpart[:, b, 2, :], rest[:], kpart[:, b, 1, :], ALU.subtract)\
                  .then_inc(parts_made, 1)

            for c in range(QC):
                dve.wait_ge(q_ready, c + 1)
            chain(nc.vector.tensor_copy(qpart[:, 0, :], qT))
            chain(nc.vector.tensor_tensor(q_rest, qT, qpart[:, 0, :], ALU.subtract))
            chain(nc.vector.tensor_copy(qpart[:, 1, :], q_rest))
            nc.vector.tensor_tensor(qpart[:, 2, :], q_rest, qpart[:, 1, :], ALU.subtract).then_inc(qpart_ready, 3)
            nc.vector.tensor_scalar(q_pos, qT, 0.0, None, ALU.max)
            chain(nc.vector.tensor_scalar(q_neg, qT, 0.0, None, ALU.min))

            with dve.Fori(0, BODY_CHUNKS // 2) as j:
                for b in range(2):
                    split_chunk(2 * j + b, j, b)
            split_chunk(BODY_CHUNKS, BODY_CHUNKS // 2, 0)

            def split_general(c):
                n = slice(c * BANK, (c + 1) * BANK)
                k = 3 * c
                nc.vector.tensor_copy(shift_part[:, 0, n], shift[:, n]).then_inc(max_split, 1)
                dve.wait_ge(max_split, k + 1)
                nc.vector.tensor_tensor(shift_rest[:, n], shift[:, n], shift_part[:, 0, n], ALU.subtract)\
                  .then_inc(max_split, 1)
                dve.wait_ge(max_split, k + 2)
                nc.vector.tensor_copy(shift_part[:, 1, n], shift_rest[:, n]).then_inc(max_split, 1)
                dve.wait_ge(max_split, k + 3)
                nc.vector.tensor_tensor(shift_part[:, 2, n], shift_rest[:, n], shift_part[:, 1, n], ALU.subtract)

            def split_shift(src, c):
                n = slice(c * BANK, (c + 1) * BANK)
                chain(nc.vector.tensor_copy(shift_part[:, 0, n], src))
                chain(nc.vector.tensor_tensor(shift_rest[:, n], src, shift_part[:, 0, n], ALU.subtract))
                chain(nc.vector.tensor_copy(shift_part[:, 1, n], shift_rest[:, n]))
                chain(nc.vector.tensor_tensor(shift_part[:, 2, n], shift_rest[:, n], shift_part[:, 1, n], ALU.subtract))

            dve.wait_ge(parts_made, PARTS * through(CHUNKS - 1))
            nc.vector.tensor_reduce(small[:, 5:6], kmax[:], AX_X, ALU.max)
            chain(nc.vector.tensor_reduce(small[:, 6:7], kmin[:], AX_X, ALU.min))
            nc.vector.tensor_scalar(bnd[:, 0, :], block, small[:, 5:6], -1.0, ALU.mult, ALU.mult)
            chain(nc.vector.tensor_scalar(bnd[:, 1, :], block, small[:, 6:7], -1.0, ALU.mult, ALU.mult))
            nc.vector.tensor_tensor(bnd[:, 2, :], bnd[:, 1, :], bnd[:, 0, :], ALU.subtract)
            nc.vector.tensor_tensor(bnd[:, 3, :], bnd[:, 0, :], bnd[:, 1, :], ALU.subtract).then_inc(bnd_ready, 1)
            for c in range(QC):
                dve.wait_ge(bound_summed, c + 1)
                split_shift(banks[0:HEADS, 6 + c, :], c)
            dve.wait_ge(gap_summed, 1)
            nc.vector.tensor_reduce(small[0:HEADS, 7:8], banks[0:HEADS, 0:2, :], mybir.AxisListType.XY, ALU.max)\
              .then_inc(gap_ready, 1)
            dve.wait_ge(gap_turned, 1)
            chain(nc.vector.tensor_reduce(small[0:1, 9:10], banks[0:1, 2, 0:HEADS], AX_X, ALU.max))
            nc.vector.tensor_scalar(flag[0:1, 0:1], small[0:1, 9:10], gap_limit / SCALE, None, ALU.is_le)\
              .then_inc(flag_ready, 1)
            dve.wait_ge(flag_ready, 1)
            bounded = dve.value_load(flag[0:1, 0:1], min_val=0, max_val=1)
            with dve.If(bounded == 0):
                dve.sem_inc(max_taken, 1)
                dve.sem_inc(max_found, 1)
                with dve.Fori(0, HEADS) as h:
                    with dve.Fori(0, QT) as t:
                        for lot in range(3):
                            k = 3 * (QT * h + t) + lot
                            dve.wait_ge(max_scores_ready, k + 1)
                            dve.wait_ge(max_found, QT * h + t + 1)
                            src = banks[:, 0:6, :] if lot < 2 else banks[:, 0, 0:ATT_K - 12 * BANK]
                            nc.vector.tensor_reduce(small[:, 10 + lot:11 + lot], src,
                                                    mybir.AxisListType.XY if lot < 2 else AX_X, ALU.max)\
                              .then_inc(max_taken, 1)
                        dve.wait_ge(max_taken, 3 * (QT * h + t) + 4)
                        nc.vector.tensor_reduce(qmax[:, bass.ds(t, 1), bass.ds(h, 1)], small[:, 10:13], AX_X, ALU.max)\
                          .then_inc(max_found, 1)
                dve.wait_ge(max_turned, 1)
                for c in range(QC):
                    n = slice(c * BANK, (c + 1) * BANK)
                    nc.vector.tensor_scalar(shift[:, n], banks[0:HEADS, 6 + c, :], -1.0, None, ALU.mult)\
                      .then_inc(max_ready, 1)
                    dve.wait_ge(max_ready, c + 1)
                    split_general(c)
            nc.vector.memset(small[0:1, 8:9], 0.0).then_inc(shift_ready, 1)

            nc.vector.memset(banks[:, 6, :], 0.0)
            nc.vector.memset(v_step[:], 0.0).then_inc(v_staged, 1)

            def stage(pair, step):
                nc.vector.tensor_copy(v_step[:], v_all[:, bass.ds(STEP_T * step, STEP_T), bass.ds(2 * pair, 2), :])\
                  .then_inc(v_staged, 1)

            def take_sums(pair, j, s):
                dve.wait_ge(o_stored[s], STORE * (j + 1))
                nc.vector.tensor_copy(o_sb[:, s, :], banks[:, 6, :]).then_inc(o_copied, 1)
                dve.wait_ge(o_copied, pair + 1)

            def invert_sums(pair, s):
                nc.vector.tensor_scalar(r_sb[:, s, :], o_sb[:, s, :], 1e-30, None, ALU.max).then_inc(o_floored, 1)
                dve.wait_ge(o_floored, pair + 1)
                nc.vector.reciprocal(r_sb[:, s, :], r_sb[:, s, :]).then_inc(sums_ready, 1)

            chain(nc.vector.tensor_tensor(x_in[:], x_in[:], bo_b[:].unsqueeze(1).to_broadcast([P, QT, DIM]), ALU.add))
            dve.wait_ge(bias_projected, 1)
            chain(nc.vector.tensor_copy(bo_b[:], banks[:, 7, 0:DIM]))
            chain(nc.vector.tensor_tensor(x_in[:], x_in[:], bo_b[:].unsqueeze(1).to_broadcast([P, QT, DIM]), ALU.add))
            nc.vector.memset(wdown[:, 0, :, :], 0.0)
            nc.vector.memset(gate[:, :, 0:1], 0.0)
            with dve.Fori(0, PAIRS // 2) as j:
                for s in range(2):
                    pair = 2 * j + s
                    dve.wait_ge(step_summed, STEPS * pair + 1)
                    take_sums(pair, j, s)
                    nc.vector.memset(banks[:, 6, :], 0.0)
                    stage(pair, 0)
                    invert_sums(pair, s)
                    with dve.Fori(1, STEPS) as step:
                        dve.wait_ge(step_summed, STEPS * pair + step + 1)
                        stage(pair, step)
            dve.wait_ge(step_summed, STEPS * PAIRS + 1)
            take_sums(PAIRS, PAIRS // 2, 0)
            invert_sums(PAIRS, 0)

            for c in range(QC):
                n = slice(c * BANK, (c + 1) * BANK)
                dve.wait_ge(attn_loaded[c], 32)
                nc.vector.tensor_tensor(attnT[:, n], attn_raw[:, n], den_b[:, n], ALU.mult).then_inc(attn_ready, 1)
            nc.vector.memset(hT[1], 0.0).then_inc(h_ready, 2)
            for c in range(QC):
                dve.wait_ge(out_projected, c + 1)
                ins = nc.vector.tensor_tensor(tiles(x1)[:, 4 * c:4 * c + 4, :],
                                              banks[:, c, :].rearrange("p (t d) -> p t d", d=DIM),
                                              x_in[:, 4 * c:4 * c + 4, :], ALU.add)
            chain(ins)
            x_stats(tiles(x1))
            dve.wait_ge(sd_ready, 3 + STAT_GROUPS)
            x8 = slice(0, QT)
            chain(nc.vector.reciprocal(rstd[:, x8], sd[:, x8]))
            chain(nc.vector.tensor_tensor(tmp[:, 1, x8], tmp[:, 0, x8], rstd[:, x8], ALU.mult))
            nc.vector.tensor_tensor(tmp[:, 2, x8], tmp[:, 1, x8], rstd[:, x8], ALU.mult).then_inc(squares_ready, 1)
            normed(tiles(x1), tiles(zf))
            dve.wait_ge(sd_ready, 4 + STAT_GROUPS)
            chain(nc.vector.reciprocal(rstd[:, QT:2 * QT], sd[:, QT:2 * QT]))
            for t in range(QT):
                ins = nc.vector.tensor_scalar(tiles(xs)[:, t, :], tiles(zf)[:, t, :], rstd[:, QT + t:QT + t + 1],
                                              None, ALU.mult)
                if t % 4 == 3:
                    ins.then_inc(xs_ready, 1)
            nc.vector.tensor_tensor(acc, x1, zf, ALU.add)
            dve.wait_ge(routed, 1)
            chain(nc.vector.tensor_copy(sc8[:], banks[:, 4, 0:QT * 8].rearrange("p (t e) -> p t e", e=8)))
            for t in range(QT):
                ins = nc.vector.max(top8[:, t, :], sc8[:, t, :])
            chain(ins)
            nc.vector.tensor_tensor(wt2[:, :, 0], top8[:, :, 1], top8[:, :, 0], ALU.subtract).then_inc(top_ready, 1)
            for t in range(QT):
                ins = nc.vector.max_index(idx8[:, t, :], top8[:, t, :], sc8[:, t, :])
            chain(ins)
            chain(nc.vector.tensor_copy(idxf[:], idx8[:, :, 0:2]))
            dve.wait_ge(ratio_ready, 1)
            chain(nc.vector.tensor_scalar(wt2[:, :, 2], wt2[:, :, 1], 1.0, None, ALU.add))
            chain(nc.vector.reciprocal(wt2[:, :, 2], wt2[:, :, 2]))
            nc.vector.tensor_tensor(wt2[:, :, 3], wt2[:, :, 1], wt2[:, :, 2], ALU.mult)
            every = [P, QT, EXPERTS]
            for k in range(2):
                chain(nc.vector.tensor_tensor(pick[:, k, :, :], iota8.unsqueeze(1).to_broadcast(every),
                                              idxf[:, :, k:k + 1].to_broadcast(every), ALU.is_equal))
                chain(nc.vector.tensor_tensor(pick[:, k, :, :], pick[:, k, :, :],
                                              wt2[:, :, 2 + k:3 + k].to_broadcast(every), ALU.mult))
            chain(nc.vector.tensor_tensor(gate[:, :, 1:], pick[:, 0, :, :], pick[:, 1, :, :], ALU.add))

            def hidden(r, u, half):
                dve.wait_ge(up_ready, 2 * r + u + 1)
                dve.wait_ge(silu_ready, 2 * r + u + 1)
                nc.vector.tensor_tensor(hT[half][:, u, :], banks[:, 2 * u, :], sg[:, u, :], ALU.mult)\
                  .then_inc(h_ready, 1)

            def add_expert(r, half, expert):
                dve.wait_ge(down_ready, r + 1)
                for t in range(4):
                    k = 4 * half + t
                    ins = nc.vector.scalar_tensor_tensor(
                        tiles(acc)[:, k, :], banks[:, 4 + half, t * DIM:(t + 1) * DIM], gate[:, k, bass.ds(expert, 1)],
                        tiles(acc)[:, k, :], ALU.mult, ALU.add)
                return ins
            with dve.Fori(0, EXPERTS) as e:
                for half in range(2):
                    hidden(2 * e + half, 0, half)
                    hidden(2 * e + half, 1, half)
                    add_expert(2 * e + half, 1 - half, e + half)
            nc.vector.memset(small[0:1, 9:10], 0.0).then_inc(acc_done, 1)
            add_expert(2 * EXPERTS, 1, EXPERTS).then_inc(acc_done, 1)

        @blk.tensor
        def _(pe):
            pe.sem_inc(turned, LEAD)
            pe.sem_inc(projected, LEAD)
            pe.wait_ge(small_loaded, 64)

            def turn(dst, src, done):
                for t in range(4):
                    ins = nc.tensor.transpose(dst[:, t * P:(t + 1) * P], src[:, t, :], ident)
                ins.then_inc(done, 1)
            for c in range(QC):
                pe.wait_ge(zq_ready, c + 1)
                turn(banks[:, c, :], tiles(q_pos)[:, 4 * c:4 * c + 4, :], zq_turned)
            pe.wait_ge(mask_counted, 1)
            nc.tensor.matmul(banks[0:1, 7, 0:1], small[0:KT, 2:3], small[0:KT, 3:4], start=True, stop=True)\
              .then_inc(mask_summed, 1)
            for c in range(QC):
                pe.wait_ge(qn_ready, c + 1)
                nc.tensor.matmul(banks[:, 2 + c, :], W(W_Q), nT[:, c, :], start=True, stop=True)\
                  .then_inc(q_projected, 1)

            def turn_chunk(i, b):
                pe.wait_ge(z_ready, i + 1)
                pe.wait_ge(n_ready, i + 1)
                turn(banks[:, b, :], z[:, b, :, :], turned)

            def project(i, b):
                pe.wait_ge(n_ready, through(i))
                pe.wait_ge(evacuated, passed(i))
                nc.tensor.matmul(banks[:, 2 + b, :], W(W_K), nT[:, b, :], start=True, stop=True)
                for t in range(4):
                    ins = nc.tensor.matmul(banks[:, 4 + b, t * P:(t + 1) * P], nT[:, b, t * P:(t + 1) * P], W(W_V),
                                           start=True, stop=True)
                ins.then_inc(projected, 1)
            pe.wait_ge(q_ready, QC)
            turn_chunk(0, 0)
            with pe.Fori(0, BODY_CHUNKS // 2) as j:
                for b in range(2):
                    turn_chunk(2 * j + b + 1, 1 - b)
                    project(2 * j + b, b)
            project(BODY_CHUNKS, 0)

            pe.wait_ge(bnd_ready, 1)
            pe.wait_ge(evacuated, through(CHUNKS - 1))
            for bank, hi, lo, done in ((6, 0, 1, bound_summed), (0, 2, 3, None)):
                for c in range(QC):
                    n = slice(c * BANK, (c + 1) * BANK)
                    nc.tensor.matmul(banks[0:HEADS, bank + c, :], bnd[:, hi, :], q_pos[:, n], start=True, stop=False)
                    ins = nc.tensor.matmul(banks[0:HEADS, bank + c, :], bnd[:, lo, :], q_neg[:, n],
                                           start=False, stop=True)
                    if done is not None:
                        ins.then_inc(done, 1)
            ins.then_inc(gap_summed, 1)
            pe.wait_ge(gap_ready, 1)
            nc.tensor.matmul(banks[0:1, 2, 0:HEADS], small[0:HEADS, 7:8], ident[0:HEADS, 0:HEADS],
                             start=True, stop=True).then_inc(gap_turned, 1)
            pe.wait_ge(qaug_loaded, 16 * PARTS * PARTS)
            pe.wait_ge(fixed_rows, 64)
            pe.wait_ge(flag_ready, 1)
            queries = qaug[:].rearrange("p h n -> p (h n)")
            bounded = pe.value_load(flag[0:1, 0:1], min_val=0, max_val=1)
            with pe.If(bounded == 0):
                pe.sem_inc(max_pair_done, 1)
                with pe.Fori(0, PAIRS) as pair:
                    for hh in range(2):
                        with pe.Fori(0, QT) as t:
                            pe.wait_ge(max_keys_loaded, 16 * KAUG_DMAS * (pair + 1))
                            at = (2 * pair + hh) * QUERIES + t * P
                            for lot in range(3):
                                pe.wait_ge(max_taken, 3 * (QT * (2 * pair + hh) + t) + lot + 1)
                                for k in range(lot * 6 * BANK, min((lot + 1) * 6 * BANK, ATT_K), BANK):
                                    w = min(BANK, ATT_K - k)
                                    ins = nc.tensor.matmul(banks[:, k // BANK % 6, 0:w], queries[:, bass.ds(at, P)],
                                                           kaug[:, 1, hh, k:k + w], start=True, stop=True)
                                ins.then_inc(max_scores_ready, 1)
                    pe.wait_ge(max_taken, 3 * QT * (2 * pair + 2) + 1)
                    pe.sem_inc(max_pair_done, 1)
                pe.wait_ge(max_found, HEADS * QT + 1)
                for t in range(QT):
                    ins = nc.tensor.matmul(banks[0:HEADS, 6 + t // 4, t % 4 * P:(t % 4 + 1) * P], qmax[:, t, :], ident,
                                           start=True, stop=True)
                ins.then_inc(max_turned, 1)

            pe.wait_ge(shift_ready, 1)
            nc.tensor.matmul(banks[:, 7, 0:DIM], C("bv").to_broadcast([P, P]), W(W_O), start=True, stop=True)\
              .then_inc(bias_projected, 1)
            pe.wait_ge(shift_loaded, 16 * PARTS)
            pe.wait_ge(probs_cleared, 1)
            pe.wait_ge(v_staged, 1)

            def scores(pair, step, s, g):
                pe.wait_ge(probs_ready, GROUPS * (STEPS * pair + step) + g + 1)
                for k in range(GROUP):
                    tile, unit = divmod(GROUP * g + k, UNITS)
                    hh, c = divmod(unit, QC)
                    ins = nc.tensor.matmul(banks[:, GROUP * (g % 2) + k, :],
                                           kaug[:, s, hh, bass.ds((STEP_T * step + tile) * P, P)],
                                           queries[:, bass.ds((2 * pair + hh) * QUERIES + c * BANK, BANK)],
                                           start=True, stop=True)
                ins.then_inc(scores_ready, 1)

            def sums(tile):
                for unit in range(UNITS):
                    at = (tile * UNITS + unit) * BANK
                    ins = nc.tensor.matmul(banks[32 * unit:32 * unit + VW, 6, :], v_step[:, tile, unit // QC, :],
                                           probs[:, at:at + BANK], start=False, stop=False, skip_group_check=True)
                return ins

            def step_of(pair, step, s, started=None):
                scores(pair, step, s, 0)
                sums(1)
                scores(pair, step, s, 1)
                sums(2).then_inc(step_summed, 1)
                scores(pair, step, s, 2)
                scores(pair, step, s, 3)
                pe.wait_ge(v_staged, STEPS * pair + step + 2)
                ins = sums(0)
                if started is not None:
                    ins.then_inc(started, 1)
            pe.sem_inc(probs_ready, 2)
            with pe.Fori(0, PAIRS // 2) as j:
                for s in range(2):
                    pe.wait_ge(keys_loaded[s], 16 * KAUG_DMAS * (j + (1 if s else CHUNKS)))
                    step_of(2 * j + s, 0, s, pair_started)
                    with pe.Fori(1, STEPS) as step:
                        step_of(2 * j + s, step, s)
            pe.wait_ge(probs_ready, GROUPS * STEPS * PAIRS + 2)
            sums(1)
            sums(2).then_inc(step_summed, 1)

            for t in range(QT):
                if t % 4 == 0:
                    pe.wait_ge(attn_ready, t // 4 + 1)
                ins = nc.tensor.matmul(banks[:, t // 4, t % 4 * P:(t % 4 + 1) * P], attnT[:, t * P:(t + 1) * P], W(W_O),
                                       start=True, stop=True)
                if t % 4 == 3:
                    ins.then_inc(out_projected, 1)
            for c in range(QC):
                pe.wait_ge(xs_ready, c + 1)
                turn(banks[:, 2 + c, :], tiles(xs)[:, 4 * c:4 * c + 4, :], xs_turned)
            pe.wait_ge(xn_ready, QC)
            for t in range(QT):
                ins = nc.tensor.matmul(banks[:, 4, t * EXPERTS:(t + 1) * EXPERTS], xnT[:, t * P:(t + 1) * P],
                                       W(W_R, EXPERTS), start=True, stop=True)
            ins.then_inc(routed, 1)

            def up(j, s, half, u):
                pe.wait_ge(h_ready, 2 * (4 * j + 2 * s + half) + u + 1)
                rhs = xnT[:, half * BANK:(half + 1) * BANK]
                nc.tensor.matmul(banks[:, 2 * u + 1, :], wup[:, s, HIDDEN + u * P:HIDDEN + (u + 1) * P], rhs,
                                 start=True, stop=True).then_inc(up_gate_ready, 1)
                return nc.tensor.matmul(banks[:, 2 * u, :], wup[:, s, u * P:(u + 1) * P], rhs,
                                        start=True, stop=True).then_inc(up_ready, 1)

            def down(half, slot):
                for t in range(4):
                    for u in range(2):
                        ins = nc.tensor.matmul(banks[:, 4 + half, t * P:(t + 1) * P], hT[half][:, u, t * P:(t + 1) * P],
                                               wdown[:, bass.ds(slot, 1), u, :], start=(u == 0), stop=(u == 1))
                ins.then_inc(down_ready, 1)
            pe.wait_ge(experts_loaded, 16)
            with pe.Fori(0, EXPERTS // 2) as j:
                for s in range(2):
                    pe.wait_ge(wup_loaded[s], 16 * (j + 1))
                    for half in range(2):
                        up(j, s, half, 0)
                        ins = up(j, s, half, 1)
                        down(1 - half, 2 * j + s + half)
            pe.wait_ge(h_ready, 4 * EXPERTS + 2)
            down(1, EXPERTS)


def kernel(**inputs):
    from concourse import bacc
    from concourse.bass_utils import run_bass_kernel_spmd

    a = {k: np.asarray(v) for k, v in inputs.items()}
    w = {k[len("L0_xattn_"):]: v for k, v in a.items() if k.startswith("L0_xattn_")}
    f = {k[len("L0_ffn_"):]: v for k, v in a.items() if k.startswith("L0_ffn_")}

    consts = np.zeros((P, C_W), np.float32)
    consts[:, C_IDENT:C_IDENT + P] = np.eye(P)
    consts[np.arange(P), C_BLOCK + np.arange(P) // HEAD] = 1.0
    consts[:, C_IOTA:C_IOTA + EXPERTS] = np.arange(EXPERTS)
    ctx = np.zeros((KT * P, DIM), np.float32)
    ctx[:KEYS] = a["ctx_1024"][0]
    mask = np.ones(KT * P, bool)
    mask[:KEYS] = a["mask_BxS2_bk0"][0]
    arrays = {
        "x": np.ascontiguousarray(a["x"][0]),
        "ctx": ctx,
        "mask": mask.reshape(KT, P),
        "consts": consts,
        "weights": np.concatenate([w["Wq"].T, w["Wk"].T, w["Wv"].T, w["Wo"].T, f["w_router"].T], 1),
        "cols": np.stack([w["qn_w"], w["qn_b"], w["cn_w"], w["cn_b"], w["bq"], w["bk"], w["bv"], f["norm_scale"]], 1),
        "bo": w["bo"],
        "w_up": np.ascontiguousarray(f["w_up"].transpose(0, 2, 1)),
        "w_down": np.ascontiguousarray(f["w_down"].reshape(EXPERTS, DIM, 2, P).transpose(3, 0, 2, 1)),
    }
    nc = bacc.Bacc("TRN2", target_bir_lowering=False, num_devices=1)
    args = [nc.dram_tensor(k, v.shape, mybir.dt.from_np(v.dtype), kind="ExternalInput").ap()
            for k, v in arrays.items()]
    out = nc.dram_tensor("out", (QUERIES, DIM), F32, kind="ExternalOutput").ap()
    build(nc, *args, out)
    r = run_bass_kernel_spmd(nc, [arrays], core_ids=[0])
    return r.results[0]["out"].reshape(1, QUERIES, DIM)
```

```python
from contextlib import ExitStack

import numpy as np

import concourse.bass as bass
from concourse import mybir
from concourse.alu_op_type import AluOpType as ALU

F32 = mybir.dt.float32
BF16 = mybir.dt.bfloat16
I32 = mybir.dt.int32
U8 = mybir.dt.uint8
U32 = mybir.dt.uint32
ACT = mybir.ActivationFunctionType
AX_X = mybir.AxisListType.X

P = 128
QUERIES, KEYS, DIM, HEADS = 1024, 6404, 128, 16
HEAD = DIM // HEADS
SCALE = HEAD ** -0.5
EXPERTS, HIDDEN = 8, 256
EPS_LN, EPS_RMS = 1e-5, 1e-6
BANK = 512
QT = QUERIES // P
QC = QUERIES // BANK
CHUNKS = -(-KEYS // BANK)
KT = CHUNKS * 4
ATT_T = -(-KEYS // P)
ATT_K = ATT_T * P
STEP_T = 3
STEPS = ATT_T // STEP_T
PAIRS = HEADS // 2
UNITS = 4
GROUP = 3
GROUPS = STEP_T * UNITS // GROUP
GW = GROUP * BANK
PARTS = 3
VW = HEAD + 1
ROW_MASK, ROW_SHIFT = 96, 97
MASKED = -1e30
HALF_RANGE = 60.0
STAT_GROUPS = 4
STAT_T = KT // STAT_GROUPS
assert ATT_T % STEP_T == 0 and KT % STAT_GROUPS == 0 and PARTS * PARTS * HEAD <= ROW_MASK

C_IDENT, C_BLOCK, C_IOTA = 0, P, P + HEADS
C_SEL = C_IOTA + EXPERTS
C_W = C_SEL + UNITS
W_Q, W_K, W_V, W_O, W_R = 0, DIM, 2 * DIM, 3 * DIM, 4 * DIM
W_W = W_R + EXPERTS
COLS = ["qn_w", "qn_b", "cn_w", "cn_b", "bq", "bk", "bv", "ns"]


def build(nc, x, ctx, mask, consts, weights, cols, bo, w_up, w_down, out, half_range=HALF_RANGE):
    kparts_dram = nc.dram_tensor("kparts_dram", [HEADS, PARTS * HEAD, KT * P], BF16).ap()
    qparts_dram = nc.dram_tensor("qparts_dram", [PARTS, DIM, QUERIES], BF16).ap()
    attn_dram = nc.dram_tensor("attn_dram", [HEADS, VW, QUERIES], F32).ap()

    with ExitStack() as es:
        def sb(name, shape, dt=F32):
            return es.enter_context(nc.sbuf_tensor(name, shape, dt))

        def sem(name):
            return es.enter_context(nc.semaphore(name))

        banks = es.enter_context(nc.psum_tensor("banks", [P, 8, BANK], F32))

        con = sb("con", [P, C_W])
        wts = sb("wts", [P, W_W])
        col = sb("col", [P, len(COLS)])
        bo_b = sb("bo_b", [P, DIM])
        x_in = sb("x_in", [P, QT, DIM])
        ctx_in = sb("ctx_in", [P, KT, DIM])
        wdown = sb("wdown", [P, EXPERTS + 1, 2, DIM])
        v_all = sb("v_all", [P, KT, HEADS, VW])
        kaug = sb("kaug", [P, 2, 2, ATT_K], BF16)
        qaug = sb("qaug", [P, HEADS, QUERIES], BF16)
        probs = sb("probs", [P, STEP_T * UNITS * BANK])
        v_step = sb("v_step", [P, STEP_T, 2, VW])
        z = sb("z", [P, 2, 4, P])
        nT = sb("nT", [P, 2, BANK])
        wup = nT
        kf = sb("kf", [P, 2, BANK])
        rest = sb("rest", [P, BANK])
        mask_f = rest[0:KT, 0:P]
        kpart = sb("kpart", [P, 2, PARTS, BANK], BF16)
        a_w = sb("a_w", [P, DIM])
        gram = sb("gram", [P, DIM])
        neg_bias = sb("neg_bias", [P, HEADS])
        st6 = sb("st6", [P, KT + QT, 6])
        mean = sb("mean", [P, KT + QT])
        tmp = sb("tmp", [P, 4, KT + QT])
        sd = sb("sd", [P, KT + QT])
        rstd = sb("rstd", [P, KT + QT])
        neg = sb("neg", [P, KT])
        small = sb("small", [P, 16])
        mask_u8 = sb("mask_u8", [KT, P], U8)
        mask_row = sb("mask_row", [KT, P], BF16)
        flag = sb("flag", [1, 2], I32)

        free = ctx_in[:].rearrange("p t d -> p (t d)")
        shift, shift_rest = free[0:HEADS, 0:QUERIES], free[0:HEADS, QUERIES:2 * QUERIES]
        shift_part = free[0:HEADS, 2 * QUERIES:4 * QUERIES].bitcast(BF16)[:, 0:PARTS * QUERIES].rearrange(
            "h (a n) -> h a n", a=PARTS)
        o_sb = free[:, 4 * QUERIES:5 * QUERIES].rearrange("p (s n) -> p s n", s=2)
        r_sb = free[:, 5 * QUERIES:6 * QUERIES].rearrange("p (s n) -> p s n", s=2)
        qmax = free[:, 6 * QUERIES:6 * QUERIES + QT * HEADS].rearrange("p (t h) -> p t h", h=HEADS)
        wo_last = free[:, 6 * QUERIES:6 * QUERIES + UNITS * DIM].rearrange("p (u d) -> p u d", u=UNITS)
        def probs_view(k, n=QUERIES):
            return probs[:, k * QUERIES:k * QUERIES + n]
        LATE = 2 * QUERIES
        zq2, bias_shift, qT, q_rest = (probs_view(k) for k in range(4))
        gram_q, bias_rest, bias_shift = zq2, zq2[0:HEADS, :], bias_shift[0:HEADS, :]
        bias_part = wdown[0:HEADS].rearrange("h e u d -> h (e u d)").bitcast(BF16)[:, 0:PARTS * QUERIES].rearrange(
            "h (a n) -> h a n", a=PARTS)
        qpart = probs[:, 4 * QUERIES:6 * QUERIES].bitcast(BF16)[:, 0:PARTS * QUERIES].rearrange(
            "p (a n) -> p a n", a=PARTS)
        late = kaug[:].rearrange("p a b n -> p (a b n)").bitcast(F32)

        def late_view(k):
            return late[:, k * QUERIES:(k + 1) * QUERIES]
        inv_b, attn_raw, attnT, x1, zf, acc, xs, xnT = (late_view(k) for k in range(8))
        hT = [late_view(k).rearrange("p (j n) -> p j n", j=2) for k in (8, 10)]
        sg = late_view(9).rearrange("p (b n) -> p b n", b=2)
        tiles = lambda v: v.rearrange("p (t d) -> p t d", d=DIM)
        sc8 = sb("sc8", [P, QT, 8])
        top8 = sb("top8", [P, QT, 8])
        idx8 = sb("idx8", [P, QT, 8], U32)
        idxf = sb("idxf", [P, QT, 2])
        wt2 = sb("wt2", [P, QT, 4])
        pick = sb("pick", [P, 2, QT, EXPERTS])
        gate = sb("gate", [P, QT, EXPERTS + 1])
        r_last = pick[:].rearrange("p a t e -> p (a t e)")[:, 0:4 * UNITS].rearrange("p (t u) -> p t u", u=UNITS)
        STORED = DIM - 2 * HEAD

        def W(at, n=DIM):
            return wts[:, at:at + n]

        def C(name):
            i = COLS.index(name)
            return col[:, i:i + 1]
        ident = con[:, C_IDENT:C_IDENT + P]
        block = con[:, C_BLOCK:C_BLOCK + HEADS]
        sel = con[:, C_SEL:C_SEL + UNITS]
        iota8 = con[:, C_IOTA:C_IOTA + EXPERTS]
        eps_ln, eps_rms = small[:, 0:1], small[:, 1:2]

        small_loaded = sem("small_loaded")
        x_loaded = sem("x_loaded")
        mask_loaded = sem("mask_loaded")
        ctx_loaded = [sem(f"ctx_loaded{g}") for g in range(STAT_GROUPS)]
        experts_loaded = sem("experts_loaded")
        consts_set = sem("consts_set")
        vchain = sem("vchain")
        pchain = sem("pchain")
        var_ready = sem("var_ready")
        sd_ready = sem("sd_ready")
        zq_ready = sem("zq_ready")
        zq_turned = sem("zq_turned")
        qn_ready = sem("qn_ready")
        q_projected = sem("q_projected")
        q_ready = sem("q_ready")
        qpart_ready = sem("qpart_ready")
        qparts_stored = sem("qparts_stored")
        qaug_zeroed = sem("qaug_zeroed")
        qaug_loaded = sem("qaug_loaded")
        neg_ready = sem("neg_ready")
        z_scaled = sem("z_scaled")
        z_ready = sem("z_ready")
        part1_ready = sem("part1_ready")
        turned = sem("turned")
        n_ready = sem("n_ready")
        projected = sem("projected")
        evacuated = sem("evacuated")
        parts_made = sem("parts_made")
        probs_cleared = sem("probs_cleared")
        kparts_stored = [sem(f"kparts_stored{b}") for b in range(2)]
        chunks_stored = sem("chunks_stored")
        kaug_set = sem("kaug_set")
        mask_counted = sem("mask_counted")
        mask_summed = sem("mask_summed")
        mask_ready = sem("mask_ready")
        fixed_rows = sem("fixed_rows")
        a_ready = sem("a_ready")
        gram_ready = sem("gram_ready")
        gram_set = sem("gram_set")
        gram_projected = sem("gram_projected")
        bias_summed = sem("bias_summed")
        bias_taken = sem("bias_taken")
        bias_split = sem("bias_split")
        gram_q_ready = sem("gram_q_ready")
        range_summed = sem("range_summed")
        range_ready = sem("range_ready")
        range_turned = sem("range_turned")
        flag_ready = sem("flag_ready")
        max_keys_loaded = sem("max_keys_loaded")
        max_scores_ready = sem("max_scores_ready")
        max_taken = sem("max_taken")
        max_pair_done = sem("max_pair_done")
        max_found = sem("max_found")
        max_turned = sem("max_turned")
        max_split = sem("max_split")
        max_ready = sem("max_ready")
        bias_shift_loaded = sem("bias_shift_loaded")
        max_shift_loaded = sem("max_shift_loaded")
        sums_cleared = sem("sums_cleared")
        keys_loaded = [sem(f"keys_loaded{s}") for s in range(2)]
        last_chunk_loaded = sem("last_chunk_loaded")
        pair_started = sem("pair_started")
        scores_ready = sem("scores_ready")
        probs_ready = sem("probs_ready")
        v_staged = sem("v_staged")
        step_summed = sem("step_summed")
        o_copied = sem("o_copied")
        o_floored = sem("o_floored")
        bias_projected = sem("bias_projected")
        o_stored = [sem(f"o_stored{s}") for s in range(2)]
        sums_ready = sem("sums_ready")
        wo_last_zeroed = sem("wo_last_zeroed")
        wo_last_loaded = sem("wo_last_loaded")
        last_sums = sem("last_sums")
        last_projected = sem("last_projected")
        attn_loaded = [sem(f"attn_loaded{c}") for c in range(QC)]
        attn_ready = sem("attn_ready")
        out_projected = sem("out_projected")
        squares_ready = sem("squares_ready")
        xs_ready = sem("xs_ready")
        xs_turned = sem("xs_turned")
        xn_ready = sem("xn_ready")
        routed = sem("routed")
        top_ready = sem("top_ready")
        ratio_ready = sem("ratio_ready")
        wup_loaded = [sem(f"wup_loaded{s}") for s in range(2)]
        up_gate_ready = sem("up_gate_ready")
        up_ready = sem("up_ready")
        silu_ready = sem("silu_ready")
        h_ready = sem("h_ready")
        down_ready = sem("down_ready")
        acc_done = sem("acc_done")
        out_stored = sem("out_stored")

        dram_tiles = lambda a: a.rearrange("(t p) d -> p t d", p=P)
        KAUG_DMAS = 2
        STORE = 2 * UNITS * 16

        def load_keys(eng, pair, slot, done, first=0, n=ATT_K):
            for hh in range(2):
                src = kparts_dram[bass.ds(2 * pair + hh, 1), :, bass.ds(first, n)]
                eng.dma_start(kaug[0:PARTS * PARTS * HEAD, slot, hh, bass.ds(first, n)],
                              src.to_broadcast([PARTS, PARTS * HEAD, n])).then_inc(done, 16)

        BODY_CHUNKS = CHUNKS - 1
        LEAD = 2

        def passed(i):
            return i + 1

        def through(i):
            return i + 1 + LEAD

        blk = es.enter_context(nc.Block())

        @blk.sync
        def _(sp):
            for b in range(2):
                sp.sem_inc(kparts_stored[b], 16)
            sp.dma_start(x_in[:], dram_tiles(x)).then_inc(x_loaded, 16)
            for dst, src in ((con[:], consts), (wts[:], weights), (col[:], cols),
                             (bo_b[:], bo.partition_broadcast(P))):
                sp.dma_start(dst, src).then_inc(small_loaded, 16)
            sp.dma_start(mask_u8[:], mask).then_inc(mask_loaded, 16)
            ct = dram_tiles(ctx)
            for g in range(STAT_GROUPS):
                sp.dma_start(ctx_in[:, g * STAT_T:(g + 1) * STAT_T, :],
                             ct[:, g * STAT_T:(g + 1) * STAT_T, :]).then_inc(ctx_loaded[g], 16)
            sp.wait_ge(kaug_set, 1)
            sp.wait_ge(mask_ready, 1)
            for s in range(2):
                for hh in range(2):
                    sp.dma_start(kaug[ROW_MASK:ROW_MASK + 1, s, hh, :],
                                 mask_row[0:ATT_T, :]).then_inc(fixed_rows, 16)
            sp.wait_ge(qpart_ready, 3)
            sp.dma_start(qparts_dram.rearrange("a f n -> f a n"), qpart).then_inc(qparts_stored, 16)

            def load_queries(a):
                for b in range(PARTS):
                    r = a * PARTS * HEAD + b
                    sp.dma_start(qaug[r:r + PARTS * (HEAD - 1) + 1:PARTS, :, :],
                                 qparts_dram[a].rearrange("(h d) n -> d h n", d=HEAD)).then_inc(qaug_loaded, 16)

            def store_kparts(i, b):
                sp.wait_ge(parts_made, PARTS * through(i))
                sp.dma_start(kparts_dram[:, :, bass.ds(i * BANK, BANK)].rearrange("h (d b) n -> (h d) b n", b=PARTS),
                             kpart[:, b, :, :]).then_inc(kparts_stored[b], 16)

            def load_chunk(i, j, b, n=BANK, done=keys_loaded[0]):
                sp.wait_ge(kparts_stored[b], 16 * (j + 2))
                sp.sem_inc(chunks_stored, 1)
                load_keys(sp, 0, 0, done, i * BANK, n)

            def load_shift(parts, done):
                for a in range(PARTS):
                    sp.dma_start(qaug[ROW_SHIFT + a:ROW_SHIFT + a + 1, :, :], parts[:, a, :]).then_inc(done, 16)
            store_kparts(0, 0)
            sp.wait_ge(qparts_stored, 16)
            sp.wait_ge(qaug_zeroed, 2)
            load_queries(0)
            store_kparts(1, 1)
            load_chunk(0, 0, 0)
            load_queries(1)
            store_kparts(2, 0)
            load_chunk(1, 0, 1)
            load_queries(2)
            sp.wait_ge(bias_split, 1)
            load_shift(bias_part, bias_shift_loaded)
            with sp.Fori(1, BODY_CHUNKS // 2) as j:
                for b in range(2):
                    store_kparts(2 * j + b + 1, 1 - b)
                    load_chunk(2 * j + b, j, b)
            load_chunk(BODY_CHUNKS, BODY_CHUNKS // 2, 0, ATT_K - BODY_CHUNKS * BANK, last_chunk_loaded)
            sp.wait_ge(chunks_stored, CHUNKS)
            sp.wait_ge(bias_shift_loaded, 16 * PARTS)
            for s in range(2):
                sp.dma_start(wup[:, s, :], w_up[s]).then_inc(wup_loaded[s], 16)
            sp.dma_start(wdown[:, 1:, :, :], w_down).then_inc(experts_loaded, 16)
            sp.wait_ge(flag_ready, 1)
            bounded = sp.value_load(flag[0:1, 0:1], min_val=0, max_val=1)
            with sp.If(bounded == 0):
                with sp.Fori(0, PAIRS) as pair:
                    sp.wait_ge(max_pair_done, pair + 1)
                    load_keys(sp, pair, 1, max_keys_loaded)
                sp.wait_ge(max_pair_done, PAIRS + 1)
                sp.wait_ge(max_split, 4 * QC)
                load_shift(shift_part, max_shift_loaded)
            load_keys(sp, 1, 1, keys_loaded[1])

            def store_sums(pair, s):
                sp.wait_ge(sums_ready, pair + 1)
                for g in range(UNITS):
                    head, n, at = bass.ds(2 * pair + g // QC, 1), slice(g % QC * BANK, (g % QC + 1) * BANK), 32 * g
                    sp.dma_start(attn_dram[head, 0:HEAD, n], o_sb[at:at + HEAD, s, :]).then_inc(o_stored[s], 16)
                    sp.dma_start(attn_dram[head, HEAD:VW, n], r_sb[at + HEAD:at + VW, s, :]).then_inc(o_stored[s], 16)

            def reload_keys(pair, s):
                sp.wait_ge(pair_started, pair)
                load_keys(sp, pair, s, keys_loaded[s])
            store_sums(0, 0)
            sp.wait_ge(wo_last_zeroed, 1)
            for u in range(UNITS):
                head = (HEADS - 2 + u // QC) * HEAD
                sp.dma_start(wo_last[32 * u:32 * u + HEAD, u, :],
                             weights[head:head + HEAD, W_O:W_O + DIM]).then_inc(wo_last_loaded, 16)
            with sp.Fori(0, PAIRS // 2 - 1) as j:
                store_sums(2 * j + 1, 1)
                reload_keys(2 * j + 2, 0)
                store_sums(2 * j + 2, 0)
                reload_keys(2 * j + 3, 1)
            store_sums(PAIRS - 1, 1)
            for s in range(2):
                sp.wait_ge(o_stored[s], STORE * (PAIRS // 2 + 1))
            sp.wait_ge(pair_started, PAIRS)
            for c in range(QC):
                n = slice(c * BANK, (c + 1) * BANK)
                sp.dma_start(attn_raw[0:STORED, n], attn_dram[2:, 0:HEAD, n]).then_inc(attn_loaded[c], 16)
                sp.dma_start(inv_b[0:STORED, n], attn_dram[2:, HEAD:VW, n].to_broadcast([HEADS - 2, HEAD, BANK]))\
                  .then_inc(attn_loaded[c], 16)
            with sp.Fori(1, EXPERTS // 2) as j:
                for s in range(2):
                    sp.wait_ge(up_ready, 2 * QC * (2 * j + s - 1))
                    sp.dma_start(wup[:, s, :], w_up[2 * j + s]).then_inc(wup_loaded[s], 16)
            for half in range(2):
                sp.wait_ge(acc_done, half + 1)
                n = slice(half * 4, half * 4 + 4)
                sp.dma_start(dram_tiles(out)[:, n, :], tiles(acc)[:, n, :]).then_inc(out_stored, 16)
            sp.wait_ge(out_stored, 32)

        @blk.gpsimd
        def _(pool):
            links = [0]

            def chain(ins):
                links[0] += 1
                ins.then_inc(pchain, 1)
                pool.wait_ge(pchain, links[0])

            two_ones = float(np.array([0x3F803F80], np.uint32).view(np.float32)[0])
            chain(pool.memset(qaug[64:P, :, :].bitcast(F32), 0.0))
            pool.memset(qaug[ROW_MASK:ROW_MASK + 1, :, :].bitcast(F32), two_ones).then_inc(qaug_zeroed, 2)
            pool.wait_ge(qaug_zeroed, 2)
            pool.memset(kaug[64:P, :, :, :].bitcast(F32), two_ones).then_inc(kaug_set, 1)
            pool.wait_ge(kaug_set, 1)

            def norm_chunk(i, b):
                pool.wait_ge(turned, passed(i))
                each = [P, 4, DIM]
                pool.tensor_tensor(z[:, b, :, :], ctx_in[:, bass.ds(4 * i, 4), :],
                                   rstd[:, bass.ds(4 * i, 4)].unsqueeze(2).to_broadcast(each), ALU.mult)\
                    .then_inc(z_scaled, 1)
                pool.wait_ge(z_scaled, i + 1)
                pool.tensor_tensor(z[:, b, :, :], z[:, b, :, :],
                                   neg[:, bass.ds(4 * i, 4)].unsqueeze(2).to_broadcast(each), ALU.add)\
                    .then_inc(z_ready, 1)
            pool.wait_ge(neg_ready, 1)
            norm_chunk(0, 0)
            norm_chunk(1, 1)
            pool.wait_ge(neg_ready, STAT_GROUPS)
            with pool.Fori(1, BODY_CHUNKS // 2) as j:
                for b in range(2):
                    norm_chunk(2 * j + b, b)
            norm_chunk(BODY_CHUNKS, 0)
            pool.wait_ge(qparts_stored, 16)
            pool.memset(probs[:, LATE:], 0.0).then_inc(probs_cleared, 1)

        @blk.scalar
        def _(act):
            act.sem_inc(n_ready, LEAD)
            act.sem_inc(evacuated, LEAD)
            act.wait_ge(consts_set, 2)

            def deviations(n, at, cnt):
                act.wait_ge(var_ready, n)
                nc.scalar.activation(sd[:, at:at + cnt], tmp[:, 0, at:at + cnt], ACT.Sqrt, bias=eps_ln,
                                     scale=1.0 / DIM).then_inc(sd_ready, 1)
            deviations(1, KT, QT)
            deviations(2, KT, QT)
            deviations(3, 0, STAT_T)
            deviations(4, STAT_T, STAT_T)
            act.wait_ge(small_loaded, 64)
            for c in range(QC):
                act.wait_ge(zq_turned, c + 1)
                nc.scalar.activation(nT[:, c, :], banks[:, c, :], ACT.Identity, bias=C("qn_b"), scale=C("qn_w"))\
                  .then_inc(qn_ready, 1)
            for c in range(QC):
                act.wait_ge(q_projected, c + 1)
                nc.scalar.activation(qT[:, c * BANK:(c + 1) * BANK], banks[:, 2 + c, :], ACT.Identity, bias=C("bq"))\
                  .then_inc(q_ready, 1)

            for g in range(2, STAT_GROUPS):
                deviations(3 + g, g * STAT_T, STAT_T)

            def affine(i, b):
                act.wait_ge(turned, through(i))
                act.wait_ge(projected, passed(i))
                nc.scalar.activation(nT[:, b, :], banks[:, b, :], ACT.Identity, bias=C("cn_b"), scale=C("cn_w"))\
                  .then_inc(n_ready, 1)

            def evacuate(i, j, b):
                act.wait_ge(projected, through(i))
                act.wait_ge(parts_made, PARTS * passed(i))
                nc.scalar.activation(kf[:, b, :], banks[:, 2 + b, :], ACT.Identity, bias=C("bk"))
                act.wait_ge(kparts_stored[b], 16 * (j + 1))
                nc.scalar.activation(kpart[:, b, 0, :], banks[:, 2 + b, :], ACT.Identity, bias=C("bk"))\
                  .then_inc(part1_ready, 1)
                nc.scalar.activation(v_all[:, bass.ds(4 * i, 4), :, 0:HEAD],
                                     banks[:, 4 + b, :].rearrange("p (t h d) -> p t h d", t=4, d=HEAD),
                                     ACT.Copy).then_inc(evacuated, 1)
            affine(0, 0)
            with act.Fori(0, BODY_CHUNKS // 2) as j:
                for b in range(2):
                    affine(2 * j + b + 1, 1 - b)
                    evacuate(2 * j + b, j, b)
            evacuate(BODY_CHUNKS, BODY_CHUNKS // 2, 0)

            act.preload_act_table(ACT.Exp)
            with act.Fori(0, PAIRS * STEPS) as it:
                for g in range(GROUPS):
                    s = GROUP * (g % 2)
                    act.wait_ge(scores_ready, GROUPS * it + g + 1)
                    nc.scalar.activation(probs[:, g * GW:(g + 1) * GW].rearrange("p (b n) -> p b n", n=BANK),
                                         banks[:, s:s + GROUP, :], ACT.Exp, scale=SCALE).then_inc(probs_ready, 1)

            deviations(3 + STAT_GROUPS, 0, QT)
            act.wait_ge(squares_ready, 1)
            nc.scalar.activation(sd[:, QT:2 * QT], tmp[:, 2, 0:QT], ACT.Sqrt, bias=eps_rms, scale=1.0 / DIM)\
              .then_inc(sd_ready, 1)
            for c in range(QC):
                act.wait_ge(xs_turned, c + 1)
                nc.scalar.activation(xnT[:, c * BANK:(c + 1) * BANK], banks[:, 2 + c, :], ACT.Copy, scale=C("ns"))\
                  .then_inc(xn_ready, 1)
            act.wait_ge(top_ready, 1)
            nc.scalar.activation(wt2[:, :, 1], wt2[:, :, 0], ACT.Exp).then_inc(ratio_ready, 1)
            act.preload_act_table(ACT.Silu)
            with act.Fori(0, 2 * EXPERTS) as r:
                for u in range(2):
                    act.wait_ge(up_gate_ready, 2 * r + u + 1)
                    nc.scalar.activation(sg[:, u, :], banks[:, 2 * u + 1, :], ACT.Silu).then_inc(silu_ready, 1)

        @blk.vector
        def _(dve):
            links = [0]

            def chain(ins):
                links[0] += 1
                ins.then_inc(vchain, 1)
                dve.wait_ge(vchain, links[0])

            dve.memset(eps_ln, EPS_LN).then_inc(consts_set, 1)
            dve.memset(eps_rms, EPS_RMS).then_inc(consts_set, 1)
            dve.sem_inc(parts_made, PARTS * LEAD)
            dve.sem_inc(o_stored[0], STORE)
            dve.sem_inc(o_stored[1], STORE)

            def moments(at, cnt):
                s = slice(at, at + cnt)
                me, ve, mo, vo = (st6[:, s, k] for k in (1, 2, 4, 5))
                nc.vector.tensor_tensor(tmp[:, 0, s], ve, vo, ALU.add)
                nc.vector.tensor_tensor(tmp[:, 1, s], me, mo, ALU.add)
                chain(nc.vector.tensor_tensor(tmp[:, 2, s], me, mo, ALU.subtract))
                nc.vector.tensor_scalar(mean[:, s], tmp[:, 1, s], 0.5, None, ALU.mult)
                chain(nc.vector.scalar_tensor_tensor(tmp[:, 3, s], tmp[:, 2, s], DIM / 4.0, tmp[:, 2, s],
                                                     ALU.mult, ALU.mult))
                nc.vector.tensor_tensor(tmp[:, 0, s], tmp[:, 0, s], tmp[:, 3, s], ALU.add).then_inc(var_ready, 1)

            def stats(src, at, cnt=QT):
                for t in range(cnt):
                    ins = nc.vector.bn_stats(st6[:, at + t, :], src[:, t, :])
                chain(ins)
                moments(at, cnt)

            def key_stats(g):
                dve.wait_ge(ctx_loaded[g], 16)
                stats(ctx_in[:, g * STAT_T:(g + 1) * STAT_T, :], g * STAT_T, STAT_T)

            def key_scales(g):
                s = slice(g * STAT_T, (g + 1) * STAT_T)
                dve.wait_ge(sd_ready, 3 + g)
                chain(nc.vector.reciprocal(rstd[:, s], sd[:, s]))
                nc.vector.scalar_tensor_tensor(neg[:, s], mean[:, s], -1.0, rstd[:, s], ALU.mult, ALU.mult)\
                  .then_inc(neg_ready, 1)

            def normed(src, dst, at, each=None):
                for t in range(QT):
                    k = slice(at + t, at + t + 1)
                    ins = nc.vector.tensor_scalar(dst[:, t, :], src[:, t, :], mean[:, k], rstd[:, k],
                                                  ALU.subtract, ALU.mult)
                    if each is not None and t % 4 == 3:
                        ins.then_inc(each, 1)
                return ins

            dve.wait_ge(x_loaded, 16)
            zq = tiles(q_rest)
            q8 = slice(KT, KT + QT)
            stats(x_in, KT)
            dve.wait_ge(sd_ready, 1)
            chain(nc.vector.reciprocal(rstd[:, q8], sd[:, q8]))
            chain(normed(x_in, zq, KT))
            stats(zq, KT)
            key_stats(0)
            dve.wait_ge(sd_ready, 2)
            chain(nc.vector.reciprocal(rstd[:, q8], sd[:, q8]))
            normed(zq, tiles(zq2), KT, each=zq_ready)
            key_scales(0)
            dve.wait_ge(small_loaded, 64)
            nc.vector.tensor_scalar(a_w[:], W(W_K), C("cn_w"), None, ALU.mult).then_inc(a_ready, 1)
            key_stats(1)
            key_scales(1)
            dve.wait_ge(mask_loaded, 16)
            chain(nc.vector.tensor_copy(mask_f, mask_u8[:]))
            chain(nc.vector.tensor_reduce(small[0:KT, 2:3], mask_f, AX_X, ALU.add))
            nc.vector.memset(small[:, 3:4], 1.0).then_inc(mask_counted, 1)
            dve.wait_ge(mask_summed, 1)
            chain(nc.vector.tensor_scalar(small[0:1, 4:5], banks[0:1, 7, 0:1], KT * P - 0.5, None, ALU.is_lt))
            chain(nc.vector.tensor_tensor(mask_f[0:1, 0:1], mask_f[0:1, 0:1], small[0:1, 4:5], ALU.mult))
            nc.vector.tensor_scalar(mask_row[:], mask_f, MASKED, None, ALU.mult).then_inc(mask_ready, 1)
            dve.wait_ge(gram_ready, 1)
            nc.vector.tensor_tensor(gram[:].rearrange("p (h d) -> p h d", d=HEAD),
                                    banks[:, 6, 0:DIM].rearrange("p (h d) -> p h d", d=HEAD),
                                    block.unsqueeze(2).to_broadcast([P, HEADS, HEAD]), ALU.mult)
            chain(nc.vector.tensor_tensor(small[:, 5:6], banks[:, 6, DIM:DIM + 1], C("bk"), ALU.add))
            nc.vector.tensor_scalar(neg_bias[:], block, small[:, 5:6], -1.0, ALU.mult, ALU.mult).then_inc(gram_set, 1)
            for g in range(2, STAT_GROUPS):
                key_stats(g)
            for g in range(2, STAT_GROUPS):
                key_scales(g)
            nc.vector.memset(v_all[:, :, :, HEAD:VW], 1.0)

            def split_chunk(i, j, b):
                dve.wait_ge(part1_ready, i + 1)
                dve.wait_ge(parts_made, PARTS * through(i - 1))
                nc.vector.tensor_tensor(rest[:], kf[:, b, :], kpart[:, b, 0, :], ALU.subtract).then_inc(parts_made, 1)
                dve.wait_ge(parts_made, PARTS * through(i) - 2)
                nc.vector.tensor_copy(kpart[:, b, 1, :], rest[:]).then_inc(parts_made, 1)
                dve.wait_ge(parts_made, PARTS * through(i) - 1)
                nc.vector.tensor_tensor(kpart[:, b, 2, :], rest[:], kpart[:, b, 1, :], ALU.subtract)\
                  .then_inc(parts_made, 1)

            dve.wait_ge(q_ready, QC)
            dve.wait_ge(gram_projected, 1)
            nc.vector.tensor_tensor(gram_q.rearrange("p (c n) -> p c n", c=QC), banks[:, 6:8, :],
                                    qT.rearrange("p (c n) -> p c n", c=QC), ALU.mult).then_inc(gram_q_ready, 1)
            dve.wait_ge(bias_summed, 1)
            nc.vector.tensor_copy(bias_shift.rearrange("p (c n) -> p c n", c=QC), banks[0:HEADS, 4:6, :])\
              .then_inc(bias_taken, 1)
            chain(nc.vector.tensor_copy(qpart[:, 0, :], qT))
            chain(nc.vector.tensor_tensor(q_rest, qT, qpart[:, 0, :], ALU.subtract))
            chain(nc.vector.tensor_copy(qpart[:, 1, :], q_rest))
            nc.vector.tensor_tensor(qpart[:, 2, :], q_rest, qpart[:, 1, :], ALU.subtract).then_inc(qpart_ready, 3)
            dve.wait_ge(range_summed, 1)
            nc.vector.tensor_reduce(small[0:HEADS, 7:8], banks[0:HEADS, 6:8, :], mybir.AxisListType.XY, ALU.max)\
              .then_inc(range_ready, 1)
            split_chunk(0, 0, 0)
            split_chunk(1, 0, 1)
            dve.wait_ge(bias_taken, 1)
            chain(nc.vector.tensor_copy(bias_part[:, 0, :], bias_shift))
            chain(nc.vector.tensor_tensor(bias_rest, bias_shift, bias_part[:, 0, :], ALU.subtract))
            chain(nc.vector.tensor_copy(bias_part[:, 1, :], bias_rest))
            nc.vector.tensor_tensor(bias_part[:, 2, :], bias_rest, bias_part[:, 1, :], ALU.subtract)\
              .then_inc(bias_split, 1)

            with dve.Fori(1, BODY_CHUNKS // 2) as j:
                for b in range(2):
                    split_chunk(2 * j + b, j, b)
            split_chunk(BODY_CHUNKS, BODY_CHUNKS // 2, 0)

            def split_shift(c):
                n = slice(c * BANK, (c + 1) * BANK)
                k = 4 * c
                nc.vector.tensor_copy(shift_part[:, 0, n], shift[:, n]).then_inc(max_split, 1)
                dve.wait_ge(max_split, k + 1)
                nc.vector.tensor_tensor(shift_rest[:, n], shift[:, n], shift_part[:, 0, n], ALU.subtract)\
                  .then_inc(max_split, 1)
                dve.wait_ge(max_split, k + 2)
                nc.vector.tensor_copy(shift_part[:, 1, n], shift_rest[:, n]).then_inc(max_split, 1)
                dve.wait_ge(max_split, k + 3)
                nc.vector.tensor_tensor(shift_part[:, 2, n], shift_rest[:, n], shift_part[:, 1, n], ALU.subtract)\
                  .then_inc(max_split, 1)

            dve.wait_ge(range_turned, 1)
            chain(nc.vector.tensor_reduce(small[0:1, 9:10], banks[0:1, 6, 0:HEADS], AX_X, ALU.max))
            nc.vector.tensor_scalar(flag[0:1, 0:1], small[0:1, 9:10], half_range * abs(half_range) / SCALE ** 2 / DIM,
                                    None, ALU.is_le).then_inc(flag_ready, 1)
            dve.wait_ge(flag_ready, 1)
            bounded = dve.value_load(flag[0:1, 0:1], min_val=0, max_val=1)
            with dve.If(bounded == 0):
                dve.sem_inc(max_taken, 1)
                dve.sem_inc(max_found, 1)
                with dve.Fori(0, HEADS) as h:
                    with dve.Fori(0, QT) as t:
                        for lot in range(3):
                            k = 3 * (QT * h + t) + lot
                            dve.wait_ge(max_scores_ready, k + 1)
                            dve.wait_ge(max_found, QT * h + t + 1)
                            src = banks[:, 0:6, :] if lot < 2 else banks[:, 0, 0:ATT_K - 12 * BANK]
                            nc.vector.tensor_reduce(small[:, 10 + lot:11 + lot], src,
                                                    mybir.AxisListType.XY if lot < 2 else AX_X, ALU.max)\
                              .then_inc(max_taken, 1)
                        dve.wait_ge(max_taken, 3 * (QT * h + t) + 4)
                        nc.vector.tensor_reduce(qmax[:, bass.ds(t, 1), bass.ds(h, 1)], small[:, 10:13], AX_X, ALU.max)\
                          .then_inc(max_found, 1)
                dve.wait_ge(max_turned, 1)
                for c in range(QC):
                    n = slice(c * BANK, (c + 1) * BANK)
                    nc.vector.tensor_tensor(shift[:, n], bias_shift[:, n], banks[0:HEADS, 6 + c, :], ALU.subtract)\
                      .then_inc(max_ready, 1)
                    dve.wait_ge(max_ready, c + 1)
                    split_shift(c)

            nc.vector.memset(banks[:, 6, :], 0.0).then_inc(sums_cleared, 1)
            nc.vector.memset(v_step[:], 0.0).then_inc(v_staged, 1)

            def stage(pair, step):
                nc.vector.tensor_copy(v_step[:], v_all[:, bass.ds(STEP_T * step, STEP_T), bass.ds(2 * pair, 2), :])\
                  .then_inc(v_staged, 1)

            def take_sums(pair, j, s):
                dve.wait_ge(o_stored[s], STORE * (j + 1))
                nc.vector.tensor_copy(o_sb[:, s, :], banks[:, 6, :]).then_inc(o_copied, 1)
                dve.wait_ge(o_copied, pair + 1)

            def invert_sums(pair, s):
                nc.vector.tensor_scalar(r_sb[:, s, :], o_sb[:, s, :], 1e-30, None, ALU.max).then_inc(o_floored, 1)
                dve.wait_ge(o_floored, pair + 1)
                nc.vector.reciprocal(r_sb[:, s, :], r_sb[:, s, :]).then_inc(sums_ready, 1)

            chain(nc.vector.tensor_tensor(x_in[:], x_in[:], bo_b[:].unsqueeze(1).to_broadcast([P, QT, DIM]), ALU.add))
            dve.wait_ge(bias_projected, 1)
            chain(nc.vector.tensor_copy(bo_b[:], banks[:, 7, 0:DIM]))
            chain(nc.vector.tensor_tensor(x_in[:], x_in[:], bo_b[:].unsqueeze(1).to_broadcast([P, QT, DIM]), ALU.add))
            nc.vector.memset(wo_last, 0.0).then_inc(wo_last_zeroed, 1)
            nc.vector.memset(wdown[:, 0, :, :], 0.0)
            nc.vector.memset(gate[:, :, 0:1], 0.0)
            with dve.Fori(0, PAIRS // 2) as j:
                for s in range(2):
                    pair = 2 * j + s
                    dve.wait_ge(step_summed, STEPS * pair + 1)
                    take_sums(pair, j, s)
                    nc.vector.memset(banks[:, 6, :], 0.0)
                    stage(pair, 0)
                    invert_sums(pair, s)
                    with dve.Fori(1, STEPS) as step:
                        dve.wait_ge(step_summed, STEPS * pair + step + 1)
                        stage(pair, step)
            for c in range(QC):
                n = slice(c * BANK, (c + 1) * BANK)
                dve.wait_ge(attn_loaded[c], 32)
                nc.vector.tensor_tensor(attnT[0:STORED, n], attn_raw[0:STORED, n], inv_b[0:STORED, n], ALU.mult)\
                  .then_inc(attn_ready, 1)
            dve.wait_ge(step_summed, STEPS * PAIRS + 1)
            take_sums(PAIRS, PAIRS // 2, 0)
            nc.vector.memset(hT[1], 0.0).then_inc(h_ready, 2)

            for c in range(QC):
                dve.wait_ge(out_projected, c + 1)
                ins = nc.vector.tensor_tensor(tiles(x1)[:, 4 * c:4 * c + 4, :],
                                              banks[:, c, :].rearrange("p (t d) -> p t d", d=DIM),
                                              x_in[:, 4 * c:4 * c + 4, :], ALU.add)
            chain(ins)
            dve.wait_ge(last_sums, 1)
            chain(nc.vector.reciprocal(r_last, banks[:, 7, 0:4 * UNITS].rearrange("p (t u) -> p t u", u=UNITS)))
            for hh in range(2):
                for t in range(4):
                    if hh == 0:
                        dve.wait_ge(last_projected, t + 1)
                    for c in range(QC):
                        u, k = QC * hh + c, 4 * c + t
                        ins = nc.vector.scalar_tensor_tensor(
                            tiles(x1)[:, k, :], banks[:, 2 + t, u * DIM:(u + 1) * DIM], r_last[:, t, u:u + 1],
                            tiles(x1)[:, k, :], ALU.mult, ALU.add)
                chain(ins)
            stats(tiles(x1), 0)
            dve.wait_ge(sd_ready, 3 + STAT_GROUPS)
            x8 = slice(0, QT)
            chain(nc.vector.reciprocal(rstd[:, x8], sd[:, x8]))
            chain(nc.vector.tensor_tensor(tmp[:, 1, x8], tmp[:, 0, x8], rstd[:, x8], ALU.mult))
            nc.vector.tensor_tensor(tmp[:, 2, x8], tmp[:, 1, x8], rstd[:, x8], ALU.mult).then_inc(squares_ready, 1)
            dve.wait_ge(sd_ready, 4 + STAT_GROUPS)
            chain(nc.vector.reciprocal(rstd[:, QT:2 * QT], sd[:, QT:2 * QT]))
            chain(nc.vector.tensor_tensor(rstd[:, QT:2 * QT], rstd[:, QT:2 * QT], rstd[:, x8], ALU.mult))
            for t in range(QT):
                ins = nc.vector.tensor_scalar(tiles(xs)[:, t, :], tiles(x1)[:, t, :], mean[:, t:t + 1],
                                              rstd[:, QT + t:QT + t + 1], ALU.subtract, ALU.mult)
                if t % 4 == 3:
                    ins.then_inc(xs_ready, 1)
            chain(normed(tiles(x1), tiles(zf), 0))
            nc.vector.tensor_tensor(acc, x1, zf, ALU.add)
            dve.wait_ge(routed, 1)
            chain(nc.vector.tensor_copy(sc8[:], banks[:, 4, 0:QT * 8].rearrange("p (t e) -> p t e", e=8)))
            for t in range(QT):
                ins = nc.vector.max(top8[:, t, :], sc8[:, t, :])
            chain(ins)
            nc.vector.tensor_tensor(wt2[:, :, 0], top8[:, :, 1], top8[:, :, 0], ALU.subtract).then_inc(top_ready, 1)
            for t in range(QT):
                ins = nc.vector.max_index(idx8[:, t, :], top8[:, t, :], sc8[:, t, :])
            chain(ins)
            chain(nc.vector.tensor_copy(idxf[:], idx8[:, :, 0:2]))
            dve.wait_ge(ratio_ready, 1)
            chain(nc.vector.tensor_scalar(wt2[:, :, 2], wt2[:, :, 1], 1.0, None, ALU.add))
            chain(nc.vector.reciprocal(wt2[:, :, 2], wt2[:, :, 2]))
            nc.vector.tensor_tensor(wt2[:, :, 3], wt2[:, :, 1], wt2[:, :, 2], ALU.mult)
            every = [P, QT, EXPERTS]
            for k in range(2):
                chain(nc.vector.tensor_tensor(pick[:, k, :, :], iota8.unsqueeze(1).to_broadcast(every),
                                              idxf[:, :, k:k + 1].to_broadcast(every), ALU.is_equal))
                chain(nc.vector.tensor_tensor(pick[:, k, :, :], pick[:, k, :, :],
                                              wt2[:, :, 2 + k:3 + k].to_broadcast(every), ALU.mult))
            chain(nc.vector.tensor_tensor(gate[:, :, 1:], pick[:, 0, :, :], pick[:, 1, :, :], ALU.add))

            def hidden(r, u, half):
                dve.wait_ge(up_ready, 2 * r + u + 1)
                dve.wait_ge(silu_ready, 2 * r + u + 1)
                nc.vector.tensor_tensor(hT[half][:, u, :], banks[:, 2 * u, :], sg[:, u, :], ALU.mult)\
                  .then_inc(h_ready, 1)

            def add_expert(r, half, expert):
                dve.wait_ge(down_ready, r + 1)
                for t in range(4):
                    k = 4 * half + t
                    ins = nc.vector.scalar_tensor_tensor(
                        tiles(acc)[:, k, :], banks[:, 4 + half, t * DIM:(t + 1) * DIM], gate[:, k, bass.ds(expert, 1)],
                        tiles(acc)[:, k, :], ALU.mult, ALU.add)
                return ins
            with dve.Fori(0, EXPERTS) as e:
                for half in range(2):
                    hidden(2 * e + half, 0, half)
                    hidden(2 * e + half, 1, half)
                    add_expert(2 * e + half, 1 - half, e + half)
            nc.vector.memset(small[0:1, 9:10], 0.0).then_inc(acc_done, 1)
            add_expert(2 * EXPERTS, 1, EXPERTS).then_inc(acc_done, 1)

        @blk.tensor
        def _(pe):
            pe.sem_inc(turned, LEAD)
            pe.sem_inc(projected, LEAD)
            pe.wait_ge(small_loaded, 64)

            def turn(dst, src, done):
                for t in range(4):
                    ins = nc.tensor.transpose(dst[:, t * P:(t + 1) * P], src[:, t, :], ident)
                ins.then_inc(done, 1)
            for c in range(QC):
                pe.wait_ge(zq_ready, c + 1)
                turn(banks[:, c, :], tiles(zq2)[:, 4 * c:4 * c + 4, :], zq_turned)
            pe.wait_ge(a_ready, 1)
            nc.tensor.matmul(banks[:, 6, 0:DIM], a_w[:], a_w[:], start=True, stop=True)
            nc.tensor.matmul(banks[:, 6, DIM:DIM + 1], W(W_K), C("cn_b"), start=True, stop=True).then_inc(gram_ready, 1)
            pe.wait_ge(mask_counted, 1)
            nc.tensor.matmul(banks[0:1, 7, 0:1], small[0:KT, 2:3], small[0:KT, 3:4], start=True, stop=True)\
              .then_inc(mask_summed, 1)
            for c in range(QC):
                pe.wait_ge(qn_ready, c + 1)
                nc.tensor.matmul(banks[:, 2 + c, :], W(W_Q), nT[:, c, :], start=True, stop=True)\
                  .then_inc(q_projected, 1)

            def turn_chunk(i, b):
                pe.wait_ge(z_ready, i + 1)
                pe.wait_ge(n_ready, i + 1)
                turn(banks[:, b, :], z[:, b, :, :], turned)

            def project(i, b):
                pe.wait_ge(n_ready, through(i))
                pe.wait_ge(evacuated, passed(i))
                nc.tensor.matmul(banks[:, 2 + b, :], W(W_K), nT[:, b, :], start=True, stop=True)
                for t in range(4):
                    ins = nc.tensor.matmul(banks[:, 4 + b, t * P:(t + 1) * P], nT[:, b, t * P:(t + 1) * P], W(W_V),
                                           start=True, stop=True)
                ins.then_inc(projected, 1)
            pe.wait_ge(q_ready, QC)
            pe.wait_ge(gram_set, 1)
            for c in range(QC):
                ins = nc.tensor.matmul(banks[:, 6 + c, :], gram[:], qT[:, c * BANK:(c + 1) * BANK],
                                       start=True, stop=True)
            ins.then_inc(gram_projected, 1)
            for c in range(QC):
                ins = nc.tensor.matmul(banks[0:HEADS, 4 + c, :], neg_bias[:], qT[:, c * BANK:(c + 1) * BANK],
                                       start=True, stop=True)
            ins.then_inc(bias_summed, 1)
            turn_chunk(0, 0)
            pe.wait_ge(gram_q_ready, 1)
            for c in range(QC):
                ins = nc.tensor.matmul(banks[0:HEADS, 6 + c, :], block, gram_q[:, c * BANK:(c + 1) * BANK],
                                       start=True, stop=True)
            ins.then_inc(range_summed, 1)
            pe.wait_ge(bias_taken, 1)
            with pe.Fori(0, BODY_CHUNKS // 2) as j:
                for b in range(2):
                    turn_chunk(2 * j + b + 1, 1 - b)
                    project(2 * j + b, b)
            project(BODY_CHUNKS, 0)

            pe.wait_ge(range_ready, 1)
            nc.tensor.matmul(banks[0:1, 6, 0:HEADS], small[0:HEADS, 7:8], ident[0:HEADS, 0:HEADS],
                             start=True, stop=True).then_inc(range_turned, 1)
            pe.wait_ge(evacuated, through(CHUNKS - 1))
            pe.wait_ge(bias_shift_loaded, 16 * PARTS)
            pe.wait_ge(qaug_loaded, 16 * PARTS * PARTS)
            pe.wait_ge(fixed_rows, 64)
            pe.wait_ge(flag_ready, 1)
            queries = qaug[:].rearrange("p h n -> p (h n)")
            bounded = pe.value_load(flag[0:1, 0:1], min_val=0, max_val=1)
            with pe.If(bounded == 0):
                pe.sem_inc(max_pair_done, 1)
                with pe.Fori(0, PAIRS) as pair:
                    for hh in range(2):
                        with pe.Fori(0, QT) as t:
                            pe.wait_ge(max_keys_loaded, 16 * KAUG_DMAS * (pair + 1))
                            at = (2 * pair + hh) * QUERIES + t * P
                            for lot in range(3):
                                pe.wait_ge(max_taken, 3 * (QT * (2 * pair + hh) + t) + lot + 1)
                                for k in range(lot * 6 * BANK, min((lot + 1) * 6 * BANK, ATT_K), BANK):
                                    w = min(BANK, ATT_K - k)
                                    ins = nc.tensor.matmul(banks[:, k // BANK % 6, 0:w], queries[:, bass.ds(at, P)],
                                                           kaug[:, 1, hh, k:k + w], start=True, stop=True)
                                ins.then_inc(max_scores_ready, 1)
                    pe.wait_ge(max_taken, 3 * QT * (2 * pair + 2) + 1)
                    pe.sem_inc(max_pair_done, 1)
                pe.wait_ge(max_found, HEADS * QT + 1)
                for t in range(QT):
                    ins = nc.tensor.matmul(banks[0:HEADS, 6 + t // 4, t % 4 * P:(t % 4 + 1) * P], qmax[:, t, :], ident,
                                           start=True, stop=True)
                ins.then_inc(max_turned, 1)
                pe.wait_ge(max_shift_loaded, 16 * PARTS)

            nc.tensor.matmul(banks[:, 7, 0:DIM], C("bv").to_broadcast([P, P]), W(W_O), start=True, stop=True)\
              .then_inc(bias_projected, 1)
            pe.wait_ge(sums_cleared, 1)
            pe.wait_ge(probs_cleared, 1)
            pe.wait_ge(v_staged, 1)

            def scores(pair, step, s, g):
                pe.wait_ge(probs_ready, GROUPS * (STEPS * pair + step) + g + 1)
                for k in range(GROUP):
                    tile, unit = divmod(GROUP * g + k, UNITS)
                    hh, c = divmod(unit, QC)
                    ins = nc.tensor.matmul(banks[:, GROUP * (g % 2) + k, :],
                                           kaug[:, s, hh, bass.ds((STEP_T * step + tile) * P, P)],
                                           queries[:, bass.ds((2 * pair + hh) * QUERIES + c * BANK, BANK)],
                                           start=True, stop=True)
                ins.then_inc(scores_ready, 1)

            def sums(tile):
                for unit in range(UNITS):
                    at = (tile * UNITS + unit) * BANK
                    ins = nc.tensor.matmul(banks[32 * unit:32 * unit + VW, 6, :], v_step[:, tile, unit // QC, :],
                                           probs[:, at:at + BANK], start=False, stop=False, skip_group_check=True)
                return ins

            def step_of(pair, step, s, started=None, more_keys=None):
                scores(pair, step, s, 0)
                sums(1)
                scores(pair, step, s, 1)
                sums(2).then_inc(step_summed, 1)
                scores(pair, step, s, 2)
                scores(pair, step, s, 3)
                if more_keys is not None:
                    pe.wait_ge(more_keys, 16 * KAUG_DMAS)
                pe.wait_ge(v_staged, STEPS * pair + step + 2)
                ins = sums(0)
                if started is not None:
                    ins.then_inc(started, 1)
            pe.sem_inc(probs_ready, 2)
            with pe.Fori(0, PAIRS // 2) as j:
                for s in range(2):
                    pe.wait_ge(keys_loaded[s], 16 * KAUG_DMAS * (j + (1 if s else BODY_CHUNKS)))
                    step_of(2 * j + s, 0, s, pair_started, None if s else last_chunk_loaded)
                    with pe.Fori(1, STEPS) as step:
                        step_of(2 * j + s, step, s)
            pe.wait_ge(probs_ready, GROUPS * STEPS * PAIRS + 2)
            sums(1)
            sums(2).then_inc(step_summed, 1)

            for t in range(QT):
                if t % 4 == 0:
                    pe.wait_ge(attn_ready, t // 4 + 1)
                ins = nc.tensor.matmul(banks[:, t // 4, t % 4 * P:(t % 4 + 1) * P],
                                       attnT[0:STORED, t * P:(t + 1) * P], W(W_O)[0:STORED],
                                       start=True, stop=True)
                if t % 4 == 3:
                    ins.then_inc(out_projected, 1)
            pe.wait_ge(wo_last_loaded, 16 * UNITS)
            pe.wait_ge(o_copied, PAIRS + 1)
            for t in range(4):
                ins = nc.tensor.matmul(banks[:, 7, t * UNITS:(t + 1) * UNITS], o_sb[:, 0, t * P:(t + 1) * P], sel,
                                       start=True, stop=True)
            ins.then_inc(last_sums, 1)
            for t in range(4):
                nc.tensor.matmul(banks[:, 2 + t, :], o_sb[:, 0, t * P:(t + 1) * P],
                                 wo_last.rearrange("p u d -> p (u d)"), start=True, stop=True)\
                  .then_inc(last_projected, 1)
            for c in range(QC):
                pe.wait_ge(xs_ready, c + 1)
                turn(banks[:, 2 + c, :], tiles(xs)[:, 4 * c:4 * c + 4, :], xs_turned)
            pe.wait_ge(xn_ready, QC)
            for t in range(QT):
                ins = nc.tensor.matmul(banks[:, 4, t * EXPERTS:(t + 1) * EXPERTS], xnT[:, t * P:(t + 1) * P],
                                       W(W_R, EXPERTS), start=True, stop=True)
            ins.then_inc(routed, 1)

            def up(j, s, half, u):
                pe.wait_ge(h_ready, 2 * (4 * j + 2 * s + half) + u + 1)
                rhs = xnT[:, half * BANK:(half + 1) * BANK]
                nc.tensor.matmul(banks[:, 2 * u + 1, :], wup[:, s, HIDDEN + u * P:HIDDEN + (u + 1) * P], rhs,
                                 start=True, stop=True).then_inc(up_gate_ready, 1)
                return nc.tensor.matmul(banks[:, 2 * u, :], wup[:, s, u * P:(u + 1) * P], rhs,
                                        start=True, stop=True).then_inc(up_ready, 1)

            def down(half, slot):
                for t in range(4):
                    for u in range(2):
                        ins = nc.tensor.matmul(banks[:, 4 + half, t * P:(t + 1) * P], hT[half][:, u, t * P:(t + 1) * P],
                                               wdown[:, bass.ds(slot, 1), u, :], start=(u == 0), stop=(u == 1))
                ins.then_inc(down_ready, 1)
            pe.wait_ge(experts_loaded, 16)
            with pe.Fori(0, EXPERTS // 2) as j:
                for s in range(2):
                    pe.wait_ge(wup_loaded[s], 16 * (j + 1))
                    for half in range(2):
                        up(j, s, half, 0)
                        ins = up(j, s, half, 1)
                        down(1 - half, 2 * j + s + half)
            pe.wait_ge(h_ready, 4 * EXPERTS + 2)
            down(1, EXPERTS)


def kernel(**inputs):
    from concourse import bacc
    from concourse.bass_utils import run_bass_kernel_spmd

    a = {k: np.asarray(v) for k, v in inputs.items()}
    w = {k[len("L0_xattn_"):]: v for k, v in a.items() if k.startswith("L0_xattn_")}
    f = {k[len("L0_ffn_"):]: v for k, v in a.items() if k.startswith("L0_ffn_")}

    consts = np.zeros((P, C_W), np.float32)
    consts[:, C_IDENT:C_IDENT + P] = np.eye(P)
    consts[np.arange(P), C_BLOCK + np.arange(P) // HEAD] = 1.0
    consts[:, C_IOTA:C_IOTA + EXPERTS] = np.arange(EXPERTS)
    consts[32 * np.arange(UNITS) + HEAD, C_SEL + np.arange(UNITS)] = 1.0
    ctx = np.zeros((KT * P, DIM), np.float32)
    ctx[:KEYS] = a["ctx_1024"][0]
    mask = np.ones(KT * P, bool)
    mask[:KEYS] = a["mask_BxS2_bk0"][0]
    arrays = {
        "x": np.ascontiguousarray(a["x"][0]),
        "ctx": ctx,
        "mask": mask.reshape(KT, P),
        "consts": consts,
        "weights": np.concatenate([w["Wq"].T, w["Wk"].T, w["Wv"].T, w["Wo"].T, f["w_router"].T], 1),
        "cols": np.stack([w["qn_w"], w["qn_b"], w["cn_w"], w["cn_b"], w["bq"], w["bk"], w["bv"], f["norm_scale"]], 1),
        "bo": w["bo"],
        "w_up": np.ascontiguousarray(f["w_up"].transpose(0, 2, 1)),
        "w_down": np.ascontiguousarray(f["w_down"].reshape(EXPERTS, DIM, 2, P).transpose(3, 0, 2, 1)),
    }
    nc = bacc.Bacc("TRN2", target_bir_lowering=False, num_devices=1)
    args = [nc.dram_tensor(k, v.shape, mybir.dt.from_np(v.dtype), kind="ExternalInput").ap()
            for k, v in arrays.items()]
    out = nc.dram_tensor("out", (QUERIES, DIM), F32, kind="ExternalOutput").ap()
    build(nc, *args, out)
    r = run_bass_kernel_spmd(nc, [arrays], core_ids=[0])
    return r.results[0]["out"].reshape(1, QUERIES, DIM)
```
